# Optimizing a Trainium2 kernel written in Bass

```python
import numpy as np
import jax
import jax.numpy as jnp

def _softmax(x, axis=-1):
    return jax.nn.softmax(x, axis=axis)

def _gelu(x):
    return jax.nn.gelu(x, approximate=True)

def _silu(x):
    return jax.nn.silu(x)

def _sigmoid(x):
    return jax.nn.sigmoid(x)

def _layernorm(x, axis=-1, eps=1e-05):
    m = jnp.mean(x, axis=axis, keepdims=True)
    v = jnp.var(x, axis=axis, keepdims=True)
    return (x - m) / jnp.sqrt(v + eps)

def _scatter_add(tgt, idx, src, axis=0):
    return tgt.at[idx].add(src)

def _segment_sum(src, seg, n):
    return jax.ops.segment_sum(src, seg, n)
kernel_name = 'mk_adaln_ffn_d1_seqx_r4_bbe53a'

def setup_inputs(seed: int=0):
    np.random.seed(seed)
    _w = jnp.asarray

    def _rec_inputs():
        import jax
        import jax.numpy as jnp
        _rk = jax.random.key(seed)
        x = 8.748e-05 + 1 * jax.random.normal(jax.random.fold_in(_rk, 1), (8, 256, 512), jnp.float32)
        _lenS = 256 - jax.random.randint(jax.random.fold_in(_rk, 7), (8,), 0, max(1, 256 // 4) + 1, jnp.int32)
        _lenS2 = 256 - jax.random.randint(jax.random.fold_in(_rk, 8), (8,), 0, max(1, 256 // 4) + 1, jnp.int32)
        cond_2048 = -9.80646e-05 + 1.00041 * jax.random.normal(jax.random.fold_in(_rk, 11), (8, 512), jnp.float32)
        return (x, cond_2048)
    x, cond_2048 = _rec_inputs()

    def _L0_cond_setup():
        import jax, jax.numpy as jnp
        import numpy as np
        DT = 0.01
        EPSILON = 0.08
        ALPHA = 0.7
        BETA = 0.8
        CLAMP = 20.0
        B, T, N = (64, 128, 512)

        def _derivative(q, p, drive, coupling, bias):
            i_couple = jnp.tanh(q) @ coupling.T
            dq = q - q ** 3 / 3.0 - p + drive + i_couple + bias
            dp = EPSILON * (q + ALPHA - BETA * p)
            return (dq, dp)

        def _rk4_step(q, p, drive, coupling, bias):
            dq1, dp1 = _derivative(q, p, drive, coupling, bias)
            dq2, dp2 = _derivative(q + 0.5 * DT * dq1, p + 0.5 * DT * dp1, drive, coupling, bias)
            dq3, dp3 = _derivative(q + 0.5 * DT * dq2, p + 0.5 * DT * dp2, drive, coupling, bias)
            dq4, dp4 = _derivative(q + DT * dq3, p + DT * dp3, drive, coupling, bias)
            q_next = q + DT / 6.0 * (dq1 + 2 * dq2 + 2 * dq3 + dq4)
            p_next = p + DT / 6.0 * (dp1 + 2 * dp2 + 2 * dp3 + dp4)
            q_next = jnp.clip(q_next, -CLAMP, CLAMP)
            p_next = jnp.clip(p_next, -CLAMP, CLAMP)
            return (q_next, p_next)
        key = jax.random.key(seed)
        k1, k2, k3, k4 = jax.random.split(key, 4)
        return {'q0': jax.random.normal(k1, (B, N), dtype=jnp.float32), 'p0': jax.random.normal(k2, (B, N), dtype=jnp.float32), 'input_drive_seq': jax.random.normal(k3, (B, T, N), dtype=jnp.float32), 'coupling': jax.random.normal(k4, (N, N), dtype=jnp.float32) * 0.01, 'bias': jnp.zeros((N,), dtype=jnp.float32)}
    _L0_cond_all = _L0_cond_setup()
    _L0_cond_in = {k: v for k, v in _L0_cond_all.items() if k in ('coupling', 'bias')}
    del _L0_cond_all

    def _L0_ffn_setup():
        import jax, jax.numpy as jnp
        import numpy as np
        _FP4_LUT = jnp.array([0.0, 0.5, 1.0, 1.5, 2.0, 3.0, 4.0, 6.0, -0.0, -0.5, -1.0, -1.5, -2.0, -3.0, -4.0, -6.0], dtype=jnp.float32)
        GROUP_SIZE = 128
        EPS = 1e-06

        def _dequant_fp4(packed_i32, scales_f16, group_size):
            out_f, in_p = packed_i32.shape
            w = packed_i32.astype(jnp.uint32)
            shifts = jnp.arange(8, dtype=jnp.uint32) * 4
            nib = w[:, :, None] >> shifts & jnp.uint32(15)
            vals = _FP4_LUT[nib.astype(jnp.int32)].reshape(out_f, in_p * 8)
            s = scales_f16.astype(jnp.float32).T
            s_full = jnp.repeat(s, group_size, axis=1)
            return vals * s_full
        key = jax.random.key(seed)
        k1, k2, k3, k4, k5 = jax.random.split(key, 5)
        B, S, H, I = (4, 512, 512, 1408)
        x = jax.random.normal(k1, (B, S, H), dtype=jnp.float32)
        gate_up_packed = jax.random.randint(k2, (2 * I, H // 8), 0, 2147483647, dtype=jnp.int32)
        gate_up_scales = jax.random.uniform(k3, (H // GROUP_SIZE, 2 * I), dtype=jnp.float32).astype(jnp.float16)
        down_packed = jax.random.randint(k4, (H, I // 8), 0, 2147483647, dtype=jnp.int32)
        down_scales = jax.random.uniform(k5, (I // GROUP_SIZE, H), dtype=jnp.float32).astype(jnp.float16)
        return {'x': x, 'gate_up_packed': gate_up_packed, 'gate_up_scales': gate_up_scales, 'down_packed': down_packed, 'down_scales': down_scales}
    _L0_ffn_all = _L0_ffn_setup()
    _L0_ffn_in = {k: v for k, v in _L0_ffn_all.items() if k in ('gate_up_packed', 'gate_up_scales', 'down_packed', 'down_scales')}
    del _L0_ffn_all
    return {'x': x, 'cond_2048': cond_2048, 'L0_cond_coupling': _L0_cond_in['coupling'], 'L0_cond_bias': _L0_cond_in['bias'], 'L0_ffn_gate_up_packed': _L0_ffn_in['gate_up_packed'], 'L0_ffn_gate_up_scales': _L0_ffn_in['gate_up_scales'], 'L0_ffn_down_packed': _L0_ffn_in['down_packed'], 'L0_ffn_down_scales': _L0_ffn_in['down_scales']}

def reference(x, cond_2048, L0_cond_coupling, L0_cond_bias, L0_ffn_gate_up_packed, L0_ffn_gate_up_scales, L0_ffn_down_packed, L0_ffn_down_scales):
    import jax
    import jax.numpy as jnp

    def _L0_cond_ref(q0, p0, input_drive_seq, coupling, bias):
        import jax, jax.numpy as jnp
        import numpy as np
        DT = 0.01
        EPSILON = 0.08
        ALPHA = 0.7
        BETA = 0.8
        CLAMP = 20.0
        B, T, N = (64, 128, 512)

        def _derivative(q, p, drive, coupling, bias):
            i_couple = jnp.tanh(q) @ coupling.T
            dq = q - q ** 3 / 3.0 - p + drive + i_couple + bias
            dp = EPSILON * (q + ALPHA - BETA * p)
            return (dq, dp)

        def _rk4_step(q, p, drive, coupling, bias):
            dq1, dp1 = _derivative(q, p, drive, coupling, bias)
            dq2, dp2 = _derivative(q + 0.5 * DT * dq1, p + 0.5 * DT * dp1, drive, coupling, bias)
            dq3, dp3 = _derivative(q + 0.5 * DT * dq2, p + 0.5 * DT * dp2, drive, coupling, bias)
            dq4, dp4 = _derivative(q + DT * dq3, p + DT * dp3, drive, coupling, bias)
            q_next = q + DT / 6.0 * (dq1 + 2 * dq2 + 2 * dq3 + dq4)
            p_next = p + DT / 6.0 * (dp1 + 2 * dp2 + 2 * dp3 + dp4)
            q_next = jnp.clip(q_next, -CLAMP, CLAMP)
            p_next = jnp.clip(p_next, -CLAMP, CLAMP)
            return (q_next, p_next)
        drive_tbn = jnp.swapaxes(input_drive_seq, 0, 1)

        def scan_fn(carry, drive):
            q, p = carry
            q, p = _rk4_step(q, p, drive, coupling, bias)
            return ((q, p), q)
        (_, _), q_trace_tbn = jax.lax.scan(scan_fn, (q0, p0), drive_tbn)
        return jnp.swapaxes(q_trace_tbn, 0, 1)

    def _L0_ffn_ref(x, gate_up_packed, gate_up_scales, down_packed, down_scales):
        import jax, jax.numpy as jnp
        import numpy as np
        _FP4_LUT = jnp.array([0.0, 0.5, 1.0, 1.5, 2.0, 3.0, 4.0, 6.0, -0.0, -0.5, -1.0, -1.5, -2.0, -3.0, -4.0, -6.0], dtype=jnp.float32)
        GROUP_SIZE = 128
        EPS = 1e-06

        def _dequant_fp4(packed_i32, scales_f16, group_size):
            out_f, in_p = packed_i32.shape
            w = packed_i32.astype(jnp.uint32)
            shifts = jnp.arange(8, dtype=jnp.uint32) * 4
            nib = w[:, :, None] >> shifts & jnp.uint32(15)
            vals = _FP4_LUT[nib.astype(jnp.int32)].reshape(out_f, in_p * 8)
            s = scales_f16.astype(jnp.float32).T
            s_full = jnp.repeat(s, group_size, axis=1)
            return vals * s_full
        I = gate_up_packed.shape[0] // 2
        w_gu = _dequant_fp4(gate_up_packed, gate_up_scales, GROUP_SIZE)
        w_down = _dequant_fp4(down_packed, down_scales, GROUP_SIZE)
        gate_up = jnp.einsum('bsh,oh->bso', x, w_gu)
        gate, up = (gate_up[..., :I], gate_up[..., I:])
        h = jax.nn.silu(gate) * up
        y = jnp.einsum('bsi,hi->bsh', h, w_down)
        rms = jnp.sqrt(jnp.mean(y * y, axis=-1, keepdims=True) + EPS)
        return y / rms
    x = x + _L0_ffn_ref(_L0_cond_ref(cond_2048, cond_2048, x, L0_cond_coupling, L0_cond_bias), L0_ffn_gate_up_packed, L0_ffn_gate_up_scales, L0_ffn_down_packed, L0_ffn_down_scales)
    return x

_drawn_inputs = setup_inputs


def setup_inputs(seed=0):
    import zlib

    import numpy as np

    out = dict(_drawn_inputs(seed))
    spreads = {'L0_cond_bias': (0.0, 0.1)}
    factors = {}
    for name, (base, spread) in spreads.items():
        noise = np.random.default_rng([zlib.crc32(name.encode()), seed]).standard_normal(out[name].shape)
        drawn = base * np.exp(spread * noise) if base else spread * noise
        out[name] = jnp.asarray(drawn.astype(out[name].dtype))
    for name, factor in factors.items():
        out[name] = (out[name] * factor).astype(out[name].dtype)
    return out
```

```python
from contextlib import ExitStack

import numpy as np

import concourse.bass as bass
from concourse import mybir

F32 = mybir.dt.float32
F16 = mybir.dt.float16
I32 = mybir.dt.int32
ALU = mybir.AluOpType
ACT = mybir.ActivationFunctionType
AX = mybir.AxisListType

B, T, N = 8, 256, 512
I = 1408
P = 128
KT = N // P
CB = KT * B
STEPS = 16
BLOCKS = T // STEPS
STAGES = 4 * STEPS
TOK = STEPS * B
UNITS = I // P
UW = 2 * KT * P + N

DT, EPSILON, ALPHA, BETA, CLAMP = 0.01, 0.08, 0.7, 0.8, 20.0
S = 65536.0
CH = DT / 2
AH = CH * EPSILON
COEF = [CH, 2 * CH, CH / 3]
STAGE_COEF = [0, 0, 1, 2]


def linear_parts():
    r, p, q1, q2, q3, q4, one = np.eye(7)
    a, b = AH, BETA
    p2 = p + a * (q1 + ALPHA * one - b * p)
    p3 = p + a * (q2 + ALPHA * one - b * p2)
    p4 = p + 2 * a * (q3 + ALPHA * one - b * p3)
    p_next = (-p + p2 + 2 * p3 + p4 + a * (q4 + ALPHA * one - b * p4)) / 3
    return np.stack([q1 + CH * (r - p), q1 + CH * (r - p2), q1 + 2 * CH * (r - p3),
                     (-q1 + q2 + 2 * q3 + q4 + CH * (r - p4)) / 3, p_next])


LINEAR = linear_parts()
ROWS = len(LINEAR)
BY_R, BY_P, BY_Q1, BY_Q2, BY_Q3, BY_Q4, BY_ONE = range(7)
CUBE = [-COEF[STAGE_COEF[i]] / (3 * S * S) for i in range(4)]
SHIFT = [(COEF[STAGE_COEF[i]] + LINEAR[i, BY_Q1 + i]) / CUBE[i] for i in range(4)]

W_SCALE = 64.0
H_SCALE = 2.0 ** -9
Y_SCALE = W_SCALE * H_SCALE
FP4_BITS = 2.0 ** 14
EPS = 1e-6

FFN_FIRST, FFN_LAST = 4, 54


def ffn_schedule():
    order = []
    for u in range(UNITS + 1):
        if u < UNITS:
            order += [("gate_up", u, j, 1.0) for j in range(6 * KT)]
        if u >= 1:
            order += [("down", u - 1, j, N / P) for j in range(3)]
    total = sum(c for *_, c in order)
    at, done, spent = [[] for _ in range(STAGES)], {}, 0.0
    for kind, u, j, cost in order:
        s = FFN_FIRST + int(spent / total * (FFN_LAST + 1 - FFN_FIRST))
        if kind == "gate_up" and j == 6 * KT - 1:
            done[u] = s
        if kind == "down":
            s = max(s, done[u] + 5)
        at[s].append((kind, u, j))
        spent += cost
    return at, done


PE_AT, GATE_UP_AT = ffn_schedule()
LAST_DOWN = max(s for s in range(STAGES) if PE_AT[s])


def program(nc, x, drive, cond_t, coupling_t, bias_t, packed, scales, out):
    ctx = ExitStack()

    def sb(name, shape, dt=F32):
        return ctx.enter_context(nc.sbuf_tensor(name, shape, dt))

    def sem(name):
        return ctx.enter_context(nc.semaphore(name))

    with ctx:
        coup = sb("coup", [P, KT, N])
        wscan = sb("wscan", [P, 3, 2, KT, N], F16)
        hist = sb("hist", [P, KT, STEPS, B])
        q_raw = sb("q_raw", [P, KT, B])
        q_stage = [sb(f"q_stage{i}", [P, KT, B]) for i in (2, 3, 4)]
        p_state = sb("p_state", [P, KT, B])
        p_sum = sb("p_sum", [P, KT, B])
        th = sb("th", [P, KT, 2, B], F16)
        t32 = sb("t32", [P, KT, B])
        q_sq = sb("q_sq", [P, KT, B])
        q_cub = sb("q_cub", [P, KT, B])
        by = {n: sb(f"by_{n}", [P, ROWS, KT, B]) for n in ("drive", "p", "q1", "q2", "q3", "one")}
        term = sb("term", [P, ROWS, KT, B])
        sum_r = sb("sum_r", [P, ROWS, KT, B])
        sum_p = sb("sum_p", [P, ROWS, KT, B])
        sum_q1 = sb("sum_q1", [P, ROWS, KT, B])
        sum_q2 = sb("sum_q2", [P, ROWS, KT, B])
        sum_q3 = sb("sum_q3", [P, ROWS, KT, B])
        bias = sb("bias", [P, KT])
        bias_s = sb("bias_s", [P, KT, B])
        dr = sb("dr", [P, STEPS, KT, B])
        wffn = sb("wffn", [P, UNITS, 2, UW], F16)
        raw = [sb(f"raw{i}", [P, UW], I32) for i in range(2)]
        sc = [sb(f"sc{i}", [P, UW], F16) for i in range(2)]
        nib = sb("nib", [P, UW], I32)
        nib2 = sb("nib2", [P, UW], I32)
        w32 = sb("w32", [P, UW])
        shift = sb("shift", [P, 1], I32)
        xh = sb("xh", [P, KT, TOK], F16)
        xl = sb("xl", [P, KT, TOK], F16)
        silu = [sb(f"silu{i}", [P, TOK]) for i in range(2)]
        h32 = [sb(f"h32_{i}", [P, TOK]) for i in range(2)]
        hh = [sb(f"hh{i}", [P, TOK], F16) for i in range(2)]
        hl = [sb(f"hl{i}", [P, TOK], F16) for i in range(2)]
        junk = sb("junk", [P, N])
        sumsq = sb("sumsq", [P, 1])
        meansq = sb("meansq", [P, 1])
        rinv = sb("rinv", [P, 1])
        mhalf = sb("mhalf", [P, 1])
        xres = sb("xres", [P, N])
        osb = sb("osb", [P, N])

        HALF = 256
        scan_ps = ctx.enter_context(nc.psum_tensor("scan_ps", [P, 4 * HALF], F32))
        gu_ps = [ctx.enter_context(nc.psum_tensor(f"gu_ps{i}", [P, 512], F32)) for i in range(2)]
        y_ps = ctx.enter_context(nc.psum_tensor("y_ps", [P, N], F32))
        prod = scan_ps[:, 0:2 * HALF].rearrange("p (h r) -> p h r", h=2)
        local_ps = scan_ps[:, 2 * HALF:2 * HALF + CB].rearrange("p (c b) -> p c b", b=B)
        three = scan_ps[:, 0:3 * HALF].rearrange("p (k r) -> p r k", k=3)[:, 0:CB, :]
        three = three.rearrange("p (c b) k -> p c b k", b=B)

        stored = sem("stored")
        loaded = sem("loaded")
        raw_in = [sem(f"raw_in{i}") for i in range(2)]
        scan_in = sem("scan_in")
        names = ["q_ready", "tanh_hi", "tanh_32", "tanh_lo", "products", "squared", "cubed", "local_in",
                 "clipped", "pool_local", "pool_link", "dve_link", "p_ready", "r_read", "drive_hi", "drive_lo",
                 "xh_ready", "xl_ready", "gu_ready", "silu_ready", "h32_ready", "hh_ready", "hl_ready", "down_done",
                 "y_ready", "sumsq_ready", "rinv_ready", "out_ready", "xres_in", "osb_free", "dequant",
                 "dq_nib", "dq_w32", "dq_hi", "dq_lo"]
        sems = {n: sem(n) for n in names}
        first_num = min(s.num for s in sems.values())
        last_num = max(s.num for s in sems.values())
        assert last_num - first_num == len(names) - 1
        q_ready, tanh_hi, tanh_32, tanh_lo = (sems[n] for n in names[0:4])
        products, squared, cubed, local_in = (sems[n] for n in names[4:8])
        clipped, pool_local, pool_link, dve_link, p_ready, r_read, drive_hi, drive_lo = (
            sems[n] for n in names[8:16])
        xh_ready, xl_ready, gu_ready, silu_ready, h32_ready, hh_ready, hl_ready, down_done = (
            sems[n] for n in names[16:24])
        y_ready, sumsq_ready, rinv_ready, out_ready, xres_in, osb_free = (sems[n] for n in names[24:30])
        dq_nib, dq_w32, dq_hi, dq_lo = (sems[n] for n in names[31:35])

        def end_of_block():
            nc.gpsimd.sem_clear(range(first_num, last_num + 1))
            nc.all_engine_barrier()

        def gate_up(pe, u, j):
            half, r = divmod(j, 3 * KT)
            kt, which = divmod(r, 3)
            part, tokens = ((0, xh), (0, xl), (1, xh))[which]
            col = (half * KT + kt) * P
            if j == 0 and u >= 2:
                pe.wait_ge(h32_ready, u - 1)
            i = nc.tensor.matmul(gu_ps[u % 2][:, half * P:(half + 1) * P], wffn[:, u, part, col:col + P],
                                 tokens[:, kt, :], start=(r == 0), stop=(r == 3 * KT - 1))
            if j == 6 * KT - 1:
                i.then_inc(gu_ready, 1)

        def down(pe, u, j):
            if j == 0:
                pe.wait_ge(hl_ready, u + 1)
            part, h = ((0, hh), (0, hl), (1, hh))[j]
            i = nc.tensor.matmul(y_ps[:, :], h[u % 2][:, :], wffn[:, u, part, 2 * KT * P:UW],
                                 start=(u == 0 and j == 0), stop=(u == UNITS - 1 and j == 2))
            if j == 2:
                i.then_inc(down_done, 1)

        def ffn_silu(act, u):
            act.wait_ge(gu_ready, u + 1)
            if u >= 2:
                act.wait_ge(h32_ready, u - 1)
            nc.scalar.activation(silu[u % 2][:, :], gu_ps[u % 2][:, 0:P], ACT.Silu,
                                 scale=1.0 / W_SCALE).then_inc(silu_ready, 1)

        def ffn_h32(dve, u):
            dve.wait_ge(silu_ready, u + 1)
            if u >= 2:
                dve.wait_ge(hl_ready, u - 1)
            nc.vector.scalar_tensor_tensor(h32[u % 2][:, :], gu_ps[u % 2][:, P:2 * P], H_SCALE / W_SCALE,
                                           silu[u % 2][:, :], ALU.mult, ALU.mult).then_inc(h32_ready, 1)

        def ffn_hh(act, u):
            act.wait_ge(h32_ready, u + 1)
            if u >= 2:
                act.wait_ge(down_done, u - 1)
            nc.scalar.activation(hh[u % 2][:, :], h32[u % 2][:, :], ACT.Copy).then_inc(hh_ready, 1)

        def ffn_hl(dve, u):
            dve.wait_ge(hh_ready, u + 1)
            nc.vector.tensor_tensor(hl[u % 2][:, :], h32[u % 2][:, :], hh[u % 2][:, :],
                                    ALU.subtract).then_inc(hl_ready, 1)

        def hist_high(act, c):
            nc.scalar.activation(xh[:, c, :], hist[:, c].rearrange("p t b -> p (t b)"), ACT.Copy,
                                 scale=1.0 / S).then_inc(xh_ready, 1)

        def hist_low(dve, c):
            dve.wait_ge(xh_ready, c + 1)
            nc.vector.scalar_tensor_tensor(xl[:, c, :], hist[:, c].rearrange("p t b -> p (t b)"), 1.0 / S,
                                           xh[:, c, :], ALU.mult, ALU.subtract).then_inc(xl_ready, 1)

        def norm_sum(act):
            act.wait_ge(down_done, UNITS)
            nc.scalar.activation(junk[:, :], y_ps[:, :], ACT.Square,
                                 accum_out=sumsq[:, 0:1]).then_inc(sumsq_ready, 1)

        def norm_root(pool):
            pool.wait_ge(sumsq_ready, 1)
            nc.gpsimd.tensor_scalar(meansq[:, :], sumsq[:, :], 1.0 / N, EPS * Y_SCALE * Y_SCALE,
                                    ALU.mult, ALU.add).then_inc(rinv_ready, 1)
            pool.wait_ge(rinv_ready, 1)
            nc.gpsimd.tensor_tensor(rinv[:, :], meansq[:, :], mhalf[:, :], ALU.pow).then_inc(rinv_ready, 1)

        def norm_out(dve, n):
            if n == 0:
                dve.wait_ge(rinv_ready, 2)
                dve.wait_ge(xres_in, 16)
                dve.wait_ge(osb_free, 1)
            c = slice(n * P, (n + 1) * P)
            nc.vector.scalar_tensor_tensor(osb[:, c], y_ps[:, c], rinv[:, 0:1], xres[:, c],
                                           ALU.mult, ALU.add).then_inc(out_ready, 1)

        def sp_residual(sp, k):
            sp.wait_ge(stored, 16)
            sp.sem_inc(stored, -16)
            sp.sem_inc(osb_free, 1)
            sp.dma_start(xres[:, :], x_rows(x, k)).then_inc(xres_in, 16)

        def sp_store(sp, k):
            sp.wait_ge(out_ready, KT)
            sp.dma_start(x_rows(out, k), osb[:, :]).then_inc(stored, 16)

        def x_rows(ap, k):
            return ap.rearrange("b (k t) n -> k t b n", t=STEPS)[k]

        with nc.Block() as block:
            @block.sync
            def _(sp):
                sp.dma_start(coup[:, :, :], coupling_t).then_inc(scan_in, 16)
                sp.dma_start(q_raw[:, :, :], cond_t).then_inc(scan_in, 16)
                sp.dma_start(bias[:, :], bias_t).then_inc(scan_in, 16)
                sp.dma_start(dr[:, 0:8, :, :], drive[0]).then_inc(loaded, 16)
                for u in range(UNITS):
                    if u >= 2:
                        sp.wait_ge(dq_lo, u - 1)
                    words = packed[u].unsqueeze(1)
                    sp.dma_start(raw[u % 2][:, :], words.to_broadcast([P // 8, 8, UW])).then_inc(raw_in[u % 2], 16)
                    sp.dma_start(sc[u % 2][:, :], scales[u:u + 1, :].to_broadcast([P, UW])).then_inc(raw_in[u % 2], 16)
                sp.wait_ge(loaded, 16)

            @block.gpsimd
            def _(pool):
                nc.gpsimd.iota(shift[:, :], [[0, 1]], base=0, channel_multiplier=1).then_inc(pool_link, 1)
                for name, column, scale in (("drive", BY_R, S), ("p", BY_P, 1.0), ("q1", BY_Q1, 1.0),
                                            ("q2", BY_Q2, 1.0), ("q3", BY_Q3, 1.0)):
                    for row in range(ROWS):
                        nc.gpsimd.memset(by[name][:, row], float(LINEAR[row, column] * scale))
                nc.gpsimd.memset(mhalf[:, :], -0.5)

            @block.scalar
            def _(act):
                nc.scalar.preload_act_table(ACT.Silu)
                act.wait_ge(scan_in, 48)
                for n, coef in enumerate(COEF):
                    nc.scalar.activation(wscan[:, n, 0], coup[:, :, :], ACT.Copy,
                                         scale=coef * S).then_inc(tanh_hi, 1)
                for u in range(UNITS):
                    act.wait_ge(dq_w32, u + 1)
                    nc.scalar.activation(wffn[:, u, 0, :], w32[:, :], ACT.Copy).then_inc(dq_hi, 1)

            @block.vector
            def _(dve):
                count = [0]

                def link(ins):
                    count[0] += 1
                    ins.then_inc(dve_link, 1)
                    dve.wait_ge(dve_link, count[0])

                dve.wait_ge(scan_in, 48)
                nc.vector.tensor_scalar(p_state[:, :, :], q_raw[:, :, :], S, None, ALU.mult)
                nc.vector.tensor_scalar(hist[:, :, STEPS - 1, :], q_raw[:, :, :], S, None, ALU.mult)
                nc.vector.tensor_scalar(bias_s[:, :, :], bias[:, :].unsqueeze(2).to_broadcast([P, KT, B]), S, None,
                                        ALU.mult)
                dve.wait_ge(pool_link, 1)
                link(nc.vector.tensor_scalar(shift[:, :], shift[:, :], 7, 2, ALU.bitwise_and,
                                             ALU.logical_shift_left))
                link(nc.vector.tensor_copy(q_raw[:, :, :], hist[:, :, STEPS - 1, :]))
                for row in range(ROWS):
                    nc.vector.tensor_scalar(by["one"][:, row], bias_s[:, :, :], float(LINEAR[row, BY_R]),
                                            float(LINEAR[row, BY_ONE] * S), ALU.mult, ALU.add)
                for n, coef in enumerate(COEF):
                    dve.wait_ge(tanh_hi, n + 1)
                    nc.vector.scalar_tensor_tensor(wscan[:, n, 1], coup[:, :, :], coef * S, wscan[:, n, 0],
                                                   ALU.mult, ALU.subtract)
                for u in range(UNITS):
                    dve.wait_ge(raw_in[u % 2], 32 * (u // 2 + 1))
                    link(nc.vector.tensor_scalar(nib[:, :], raw[u % 2][:, :], shift[:, 0:1], 15,
                                                 ALU.logical_shift_right, ALU.bitwise_and))
                    link(nc.vector.scalar_tensor_tensor(nib2[:, :], nib[:, :], 3, nib[:, :],
                                                        ALU.logical_shift_left, ALU.bitwise_or))
                    link(nc.vector.tensor_scalar(nib[:, :], nib2[:, :], 0x47, 9, ALU.bitwise_and,
                                                 ALU.logical_shift_left))
                    fp4 = nib[:, :].bitcast(F16).rearrange("p (n two) -> p n two", two=2)[:, :, 0]
                    nc.vector.scalar_tensor_tensor(w32[:, :], fp4, FP4_BITS * W_SCALE, sc[u % 2][:, :],
                                                   ALU.mult, ALU.mult).then_inc(dq_w32, 1)
                    dve.wait_ge(dq_hi, u + 1)
                    nc.vector.tensor_tensor(wffn[:, u, 1, :], w32[:, :], wffn[:, u, 0, :],
                                            ALU.subtract).then_inc(dq_lo, 1)
                    dve.wait_ge(dq_lo, u + 1)
        end_of_block()

        def time_block(k, ffn):
            with nc.Block() as block:
                @block.sync
                def _(sp):
                    sp.dma_start(dr[:, 8:16, :, :], drive[2 * k + 1]).then_inc(drive_hi, 16)
                    if ffn:
                        sp_residual(sp, k - 1)
                    sp.wait_ge(r_read, 8)
                    sp.dma_start(dr[:, 0:8, :, :], drive[2 * k + 2]).then_inc(drive_lo, 16)
                    sp.wait_ge(drive_lo, 16)
                    if ffn:
                        sp_store(sp, k - 1)

                @block.tensor
                def _(pe):
                    for s in range(STAGES):
                        w = STAGE_COEF[s % 4]
                        pe.wait_ge(tanh_hi, s + 1)
                        for c in range(KT):
                            for kt in range(KT):
                                nc.tensor.matmul(prod[:, 0, c * B:(c + 1) * B],
                                                 wscan[:, w, 1, kt, c * P:(c + 1) * P], th[:, kt, 0, :],
                                                 start=(c == 0 and kt == 0), stop=False, skip_group_check=True)
                        pe.wait_ge(tanh_lo, s + 1)
                        for c in range(KT):
                            for kt in range(KT):
                                last = nc.tensor.matmul(prod[:, :, c * B:(c + 1) * B],
                                                        wscan[:, w, 0, kt, c * P:(c + 1) * P], th[:, kt, :, :],
                                                        start=False, stop=(c == KT - 1 and kt == KT - 1),
                                                        skip_group_check=True)
                        last.then_inc(products, 1)
                        if ffn:
                            for n, (kind, u, j) in enumerate(PE_AT[s]):
                                if kind == "gate_up" and u == 0 and j == 0:
                                    pe.wait_ge(xl_ready, KT)
                                (gate_up if kind == "gate_up" else down)(pe, u, j)

                @block.scalar
                def _(act):
                    for s in range(STAGES):
                        q = q_raw if s % 4 == 0 else q_stage[s % 4 - 1]
                        if s:
                            act.wait_ge(q_ready, s)
                        nc.scalar.activation(th[:, :, 0, :], q[:, :, :], ACT.Tanh,
                                             scale=1.0 / S).then_inc(tanh_hi, 1)
                        nc.scalar.activation(t32[:, :, :], q[:, :, :], ACT.Tanh, scale=1.0 / S).then_inc(tanh_32, 1)
                        if ffn:
                            if s < KT:
                                hist_high(act, s)
                            for u in range(UNITS):
                                if s == GATE_UP_AT[u] + 1:
                                    ffn_silu(act, u)
                                if s == GATE_UP_AT[u] + 3:
                                    ffn_hh(act, u)
                            if s == LAST_DOWN + 1:
                                norm_sum(act)

                @block.vector
                def _(dve):
                    linear = [sum_p[:, 0], sum_q1[:, 1], sum_q2[:, 2], sum_q3[:, 3]]
                    for s in range(STAGES):
                        t, i = divmod(s, 4)
                        before = hist[:, :, (t - 1) % STEPS, :]
                        q = before if i == 0 else q_stage[i - 1][:, :, :]
                        q_next = q_raw if i == 3 else q_stage[i]
                        if i == 0 and t:
                            dve.wait_ge(clipped, t)
                        elif s:
                            dve.wait_ge(q_ready, s)
                        nc.vector.tensor_tensor(q_sq[:, :, :], q, q, ALU.mult).then_inc(squared, 1)
                        dve.wait_ge(squared, s + 1)
                        nc.vector.scalar_tensor_tensor(q_cub[:, :, :], q_sq[:, :, :], SHIFT[i], q,
                                                       ALU.add, ALU.mult).then_inc(cubed, 1)
                        dve.wait_ge(tanh_32, s + 1)
                        nc.vector.tensor_tensor(th[:, :, 1, :], t32[:, :, :], th[:, :, 0, :],
                                                ALU.subtract).then_inc(tanh_lo, 1)
                        dve.wait_ge(cubed, s + 1)
                        dve.wait_ge(pool_local, s + 1)
                        nc.vector.scalar_tensor_tensor(local_ps, q_cub[:, :, :], CUBE[i], linear[i],
                                                       ALU.mult, ALU.add).then_inc(local_in, 1)
                        if i == 3:
                            nc.vector.scalar_tensor_tensor(p_sum[:, :, :], q, float(LINEAR[4, BY_Q4]),
                                                           sum_q3[:, 4], ALU.mult, ALU.add).then_inc(dve_link, 1)
                            dve.wait_ge(dve_link, t + 1)
                            nc.vector.tensor_scalar(p_state[:, :, :], p_sum[:, :, :], -CLAMP * S, CLAMP * S,
                                                    ALU.max, ALU.min).then_inc(p_ready, 1)
                        if ffn:
                            if s < KT:
                                hist_low(dve, s)
                            for u in range(UNITS):
                                if s == GATE_UP_AT[u] + 2:
                                    ffn_h32(dve, u)
                                if s == GATE_UP_AT[u] + 4:
                                    ffn_hl(dve, u)
                            if LAST_DOWN + 3 <= s < LAST_DOWN + 3 + KT:
                                norm_out(dve, s - LAST_DOWN - 3)
                        dve.wait_ge(local_in, s + 1)
                        dve.wait_ge(products, s + 1)
                        nc.vector.tensor_reduce(q_next[:, :, :], three, AX.X, ALU.add).then_inc(q_ready, 1)
                        if i == 3:
                            dve.wait_ge(q_ready, s + 1)
                            if ffn and t == 0:
                                dve.wait_ge(xl_ready, KT)
                            nc.vector.tensor_scalar(hist[:, :, t, :], q_raw[:, :, :], -CLAMP * S, CLAMP * S,
                                                    ALU.max, ALU.min).then_inc(clipped, 1)

                @block.gpsimd
                def _(pool):
                    count = [0]

                    def link(ins):
                        count[0] += 1
                        ins.then_inc(pool_link, 1)
                        pool.wait_ge(pool_link, count[0])

                    def add_times(to, x, name, base, first, signal=link):
                        rows = slice(first, ROWS)
                        wide = x.unsqueeze(1).to_broadcast([P, ROWS - first, KT, B])
                        link(nc.gpsimd.tensor_tensor(term[:, rows], wide, by[name][:, rows], ALU.mult))
                        signal(nc.gpsimd.tensor_tensor(to[:, rows], term[:, rows], base[:, rows], ALU.add))

                    def to_dve(ins):
                        ins.then_inc(pool_local, 1)
                        locals_done[0] += 1
                        pool.wait_ge(pool_local, locals_done[0])

                    locals_done = [0]
                    for t in range(STEPS):
                        if t == 8:
                            pool.wait_ge(drive_hi, 16)
                        wide = dr[:, t].unsqueeze(1).to_broadcast([P, ROWS, KT, B])
                        nc.gpsimd.tensor_tensor(term[:, :], wide, by["drive"][:, :], ALU.mult).then_inc(r_read, 1)
                        pool.wait_ge(r_read, t + 1)
                        link(nc.gpsimd.tensor_tensor(sum_r[:, :], term[:, :], by["one"][:, :], ALU.add))
                        if t:
                            pool.wait_ge(p_ready, t)
                        add_times(sum_p, p_state[:, :, :], "p", sum_r, 0, to_dve)
                        if t:
                            pool.wait_ge(clipped, t)
                        add_times(sum_q1, hist[:, :, (t - 1) % STEPS, :], "q1", sum_p, 1, to_dve)
                        pool.wait_ge(q_ready, 4 * t + 1)
                        add_times(sum_q2, q_stage[0][:, :, :], "q2", sum_q1, 2, to_dve)
                        pool.wait_ge(q_ready, 4 * t + 2)
                        add_times(sum_q3, q_stage[1][:, :, :], "q3", sum_q2, 3, to_dve)
                        if ffn and t == (LAST_DOWN + 1) // 4:
                            norm_root(pool)
            end_of_block()

        time_block(0, ffn=False)
        with nc.Block() as block:
            @block.sync
            def _(sp):
                sp.sem_inc(stored, 16)
        with nc.Fori(1, BLOCKS) as k:
            time_block(k, ffn=True)

        with nc.Block() as block:
            @block.sync
            def _(sp):
                sp_residual(sp, BLOCKS - 1)
                sp_store(sp, BLOCKS - 1)
                sp.wait_ge(stored, 16)

            @block.tensor
            def _(pe):
                pe.wait_ge(xl_ready, KT)
                for u in range(UNITS + 1):
                    if u < UNITS:
                        for j in range(6 * KT):
                            gate_up(pe, u, j)
                    if u >= 1:
                        for j in range(3):
                            down(pe, u - 1, j)

            @block.scalar
            def _(act):
                for c in range(KT):
                    hist_high(act, c)
                for u in range(UNITS):
                    ffn_silu(act, u)
                    ffn_hh(act, u)
                norm_sum(act)

            @block.vector
            def _(dve):
                for c in range(KT):
                    hist_low(dve, c)
                for u in range(UNITS):
                    ffn_h32(dve, u)
                    ffn_hl(dve, u)
                for n in range(KT):
                    norm_out(dve, n)

            @block.gpsimd
            def _(pool):
                norm_root(pool)


def kernel(x, cond_2048, L0_cond_coupling, L0_cond_bias, L0_ffn_gate_up_packed, L0_ffn_gate_up_scales,
           L0_ffn_down_packed, L0_ffn_down_scales):
    import concourse.bacc as bacc
    from concourse.bass_utils import run_bass_kernel_spmd

    x = np.asarray(x)
    halves = 2 * BLOCKS
    drive = x.reshape(B, halves, T // halves, KT, P).transpose(1, 4, 2, 3, 0)
    drive = np.concatenate([drive, drive[-1:]])
    gu = np.asarray(L0_ffn_gate_up_packed).reshape(2, UNITS, P, KT, P // 8).transpose(1, 4, 0, 3, 2)
    dn = np.asarray(L0_ffn_down_packed).reshape(N, UNITS, P // 8).transpose(1, 2, 0)
    packed = np.concatenate([gu.reshape(UNITS, P // 8, 2 * KT * P), dn], axis=2)
    gus = np.asarray(L0_ffn_gate_up_scales).reshape(KT, 2, UNITS, P).transpose(2, 1, 0, 3)
    scales = np.concatenate([gus.reshape(UNITS, 2 * KT * P), np.asarray(L0_ffn_down_scales)], axis=1)
    arrays = {
        "x": x,
        "drive": drive,
        "cond_t": np.asarray(cond_2048).reshape(B, KT, P).transpose(2, 1, 0),
        "coupling_t": np.asarray(L0_cond_coupling).reshape(N, KT, P).transpose(2, 1, 0),
        "bias_t": np.asarray(L0_cond_bias).reshape(KT, P).T,
        "packed": packed,
        "scales": scales,
    }
    arrays = {name: np.ascontiguousarray(a) for name, a in arrays.items()}
    nc = bacc.Bacc("TRN2", target_bir_lowering=False, num_devices=1)
    args = [nc.dram_tensor(name, a.shape, mybir.dt.from_np(a.dtype), kind="ExternalInput").ap()
            for name, a in arrays.items()]
    out = nc.dram_tensor("out", (B, T, N), F32, kind="ExternalOutput").ap()
    program(nc, *args, out)
    r = run_bass_kernel_spmd(nc, [arrays], core_ids=[0])
    return r.results[0]["out"]
```

```python
from contextlib import ExitStack

import numpy as np

import concourse.bass as bass
from concourse import mybir

F32 = mybir.dt.float32
F16 = mybir.dt.float16
I32 = mybir.dt.int32
ALU = mybir.AluOpType
ACT = mybir.ActivationFunctionType
AX = mybir.AxisListType

B, T, N = 8, 256, 512
I = 1408
P = 128
KT = N // P
HC = KT // 2
HB = HC * B
STEPS = 16
BLOCKS = T // STEPS
STAGES = 4 * STEPS
HS = STEPS // 2
TOK = STEPS * B
UNITS = I // P
UW = 2 * KT * P + N

DT, EPSILON, ALPHA, BETA, CLAMP = 0.01, 0.08, 0.7, 0.8, 20.0
S = 65536.0
CH = DT / 2
AH = CH * EPSILON
COEF = [CH, 2 * CH, CH / 3]
STAGE_COEF = [0, 0, 1, 2]


def linear_parts():
    r, p, q1, q2, q3, q4, one = np.eye(7)
    a, b = AH, BETA
    p2 = p + a * (q1 + ALPHA * one - b * p)
    p3 = p + a * (q2 + ALPHA * one - b * p2)
    p4 = p + 2 * a * (q3 + ALPHA * one - b * p3)
    p_next = (-p + p2 + 2 * p3 + p4 + a * (q4 + ALPHA * one - b * p4)) / 3
    return np.stack([q1 + CH * (r - p), q1 + CH * (r - p2), q1 + 2 * CH * (r - p3),
                     (-q1 + q2 + 2 * q3 + q4 + CH * (r - p4)) / 3, p_next])


LINEAR = linear_parts()
ROWS = len(LINEAR)
SUM_R_PARTS = (ROWS - 1) * KT
BY_R, BY_P, BY_Q1, BY_Q2, BY_Q3, BY_Q4, BY_ONE = range(7)
CUBE = [-COEF[STAGE_COEF[i]] / (3 * S * S) for i in range(4)]
SHIFT = [(COEF[STAGE_COEF[i]] + LINEAR[i, BY_Q1 + i]) / CUBE[i] for i in range(4)]

W_SCALE = 64.0
H_SCALE = 2.0 ** -9
Y_SCALE = W_SCALE * H_SCALE
FP4_BITS = 2.0 ** 14
EPS = 1e-6

FFN_FIRST, FFN_LAST = 4, 54


GU_PARTS = 4
DOWN_PARTS = 3


def ffn_schedule():
    order = []
    for u in range(UNITS + 1):
        if u < UNITS:
            order += [("gate_up", u, j, 1.0) for j in range(2 * GU_PARTS * KT)]
        if u >= 1:
            order += [("down", u - 1, j, N / 2 / P) for j in range(2 * DOWN_PARTS)]
    total = sum(c for *_, c in order)
    at, done, spent = [[] for _ in range(STAGES)], {}, 0.0
    for kind, u, j, cost in order:
        s = FFN_FIRST + int(spent / total * (FFN_LAST + 1 - FFN_FIRST))
        if kind == "gate_up" and j == 2 * GU_PARTS * KT - 1:
            done[u] = s
        if kind == "down":
            s = max(s, done[u] + 5)
        at[s].append((kind, u, j))
        spent += cost
    return at, done


PE_AT, GATE_UP_AT = ffn_schedule()
LAST_DOWN = max(s for s in range(STAGES) if PE_AT[s])


def program(nc, x, drive, cond_t, coupling_t, bias_t, packed, scales, out):
    ctx = ExitStack()

    def sb(name, shape, dt=F32):
        return ctx.enter_context(nc.sbuf_tensor(name, shape, dt))

    def sem(name):
        return ctx.enter_context(nc.semaphore(name))

    with ctx:
        coup = sb("coup", [P, KT, N])
        wscan = sb("wscan", [P, 3, 2, KT, N], F16)
        hist = sb("hist", [P, KT, STEPS, B])
        q_raw = sb("q_raw", [P, KT, B])
        q_stage = [sb(f"q_stage{i}", [P, KT, B]) for i in (2, 3, 4)]
        p_state = sb("p_state", [P, KT, B])
        p_sum = sb("p_sum", [P, KT, B])
        th = [sb(f"th{i}", [P, KT, 2, B], F16) for i in range(2)]
        t32 = sb("t32", [P, KT, B])
        q_sq = sb("q_sq", [P, KT, B])
        q_cub = sb("q_cub", [P, KT, B])
        by = {n: sb(f"by_{n}", [P, ROWS, KT, B]) for n in ("p", "q1", "q2", "q3")}
        constant = sb("constant", [P, ROWS, KT])
        term = sb("term", [P, ROWS, KT, B])
        sum_r = sb("sum_r", [P, STEPS, ROWS, KT, B])
        linear0 = sb("linear0", [P, KT, B])
        sum_p = sb("sum_p", [P, ROWS, KT, B])
        sum_q1 = sb("sum_q1", [P, ROWS, KT, B])
        sum_q2 = sb("sum_q2", [P, ROWS, KT, B])
        sum_q3 = sb("sum_q3", [P, ROWS, KT, B])
        bias = sb("bias", [P, KT])
        dr = sb("dr", [P, STEPS, KT, B])
        wffn = sb("wffn", [P, UNITS, 2, UW], F16)
        raw = [sb(f"raw{i}", [P, UW], I32) for i in range(2)]
        sc = [sb(f"sc{i}", [P, UW], F16) for i in range(2)]
        nib = sb("nib", [P, UW], I32)
        nib2 = sb("nib2", [P, UW], I32)
        w32 = sb("w32", [P, UW])
        shift = sb("shift", [P, 1], I32)
        xh = sb("xh", [P, KT, TOK], F16)
        xl = sb("xl", [P, KT, TOK], F16)
        silu = [sb(f"silu{i}", [P, TOK]) for i in range(2)]
        h32 = [sb(f"h32_{i}", [P, TOK]) for i in range(2)]
        hh = [sb(f"hh{i}", [P, TOK], F16) for i in range(2)]
        hl = [sb(f"hl{i}", [P, TOK], F16) for i in range(2)]
        junk = sb("junk", [P, N])
        sumsq = sb("sumsq", [P, 1])
        meansq = sb("meansq", [P, 1])
        rinv = sb("rinv", [P, 1])
        mhalf = sb("mhalf", [P, 1])
        xres = sb("xres", [P, N])
        osb = sb("osb", [P, N])

        APART = 256
        scan_ps = ctx.enter_context(nc.psum_tensor("scan_ps", [P, 6 * APART], F32))
        gu_ps = [ctx.enter_context(nc.psum_tensor(f"gu_ps{i}", [P, 512], F32)) for i in range(2)]
        y_ps = ctx.enter_context(nc.psum_tensor("y_ps", [P, N], F32))
        prod, three = [], []
        for half in range(2):
            own = scan_ps[:, half * 3 * APART:(half + 1) * 3 * APART].rearrange("p (k r) -> p k r", k=3)[:, :, 0:HB]
            prod.append(own[:, half:half + 2])
            three.append(own.rearrange("p k (c b) -> p c b k", b=B))
        local_ps = scan_ps[:, 2 * APART:4 * APART].rearrange("p (h r) -> p h r", h=2)[:, :, 0:HB]

        def halves(tile):
            return tile.rearrange("p (h c) b -> p h (c b)", h=2)

        stored = sem("stored")
        loaded = sem("loaded")
        raw_in = [sem(f"raw_in{i}") for i in range(2)]
        scan_in = sem("scan_in")
        names = ["q_ready", "tanh_hi", "tanh_32", "tanh_lo", "products", "squared", "cubed", "local_in",
                 "clipped", "pool_local", "pool_link", "dve_link", "p_ready", "sum_r_ready", "drive_hi", "drive_lo",
                 "xh_ready", "xl_ready", "gu_ready", "silu_ready", "h32_ready", "hh_ready", "hl_ready", "down_done",
                 "y_ready", "sumsq_ready", "rinv_ready", "out_ready", "xres_in", "osb_free", "dequant",
                 "dq_nib", "dq_w32", "dq_hi", "dq_lo"]
        sems = {n: sem(n) for n in names}
        first_num = min(s.num for s in sems.values())
        last_num = max(s.num for s in sems.values())
        assert last_num - first_num == len(names) - 1
        q_ready, tanh_hi, tanh_32, tanh_lo = (sems[n] for n in names[0:4])
        products, squared, cubed, local_in = (sems[n] for n in names[4:8])
        clipped, pool_local, pool_link, dve_link, p_ready, sum_r_ready, drive_hi, drive_lo = (
            sems[n] for n in names[8:16])
        xh_ready, xl_ready, gu_ready, silu_ready, h32_ready, hh_ready, hl_ready, down_done = (
            sems[n] for n in names[16:24])
        y_ready, sumsq_ready, rinv_ready, out_ready, xres_in, osb_free = (sems[n] for n in names[24:30])
        dq_nib, dq_w32, dq_hi, dq_lo = (sems[n] for n in names[31:35])

        def end_of_block():
            nc.gpsimd.sem_clear(range(first_num, last_num + 1))
            nc.all_engine_barrier()

        def gate_up(pe, u, j):
            half, r = divmod(j, GU_PARTS * KT)
            kt, which = divmod(r, GU_PARTS)
            part, tokens = ((0, xh), (0, xl), (1, xh), (1, xl))[which]
            col = (half * KT + kt) * P
            if j == 0 and u >= 2:
                pe.wait_ge(h32_ready, u - 1)
            i = nc.tensor.matmul(gu_ps[u % 2][:, half * P:(half + 1) * P], wffn[:, u, part, col:col + P],
                                 tokens[:, kt, :], start=(r == 0), stop=(r == GU_PARTS * KT - 1))
            if j == 2 * GU_PARTS * KT - 1:
                i.then_inc(gu_ready, 1)

        def down(pe, u, j):
            if j == 0:
                pe.wait_ge(hl_ready, u + 1)
            which, half = divmod(j, 2)
            part, h = ((0, hh), (0, hl), (1, hh), (1, hl))[which]
            cols = slice(half * N // 2, (half + 1) * N // 2)
            i = nc.tensor.matmul(y_ps[:, cols], h[u % 2][:, :], wffn[:, u, part, 2 * KT * P:][:, cols],
                                 start=(u == 0 and j == 0), stop=(u == UNITS - 1 and which == DOWN_PARTS - 1),
                                 skip_group_check=True)
            if j == 2 * DOWN_PARTS - 1:
                i.then_inc(down_done, 1)

        def ffn_silu(act, u):
            act.wait_ge(gu_ready, u + 1)
            if u >= 2:
                act.wait_ge(h32_ready, u - 1)
            nc.scalar.activation(silu[u % 2][:, :], gu_ps[u % 2][:, 0:P], ACT.Silu,
                                 scale=1.0 / W_SCALE).then_inc(silu_ready, 1)

        def ffn_h32(dve, u):
            dve.wait_ge(silu_ready, u + 1)
            if u >= 2:
                dve.wait_ge(hl_ready, u - 1)
            nc.vector.scalar_tensor_tensor(h32[u % 2][:, :], gu_ps[u % 2][:, P:2 * P], H_SCALE / W_SCALE,
                                           silu[u % 2][:, :], ALU.mult, ALU.mult).then_inc(h32_ready, 1)

        def ffn_hh(act, u):
            act.wait_ge(h32_ready, u + 1)
            if u >= 2:
                act.wait_ge(down_done, u - 1)
            nc.scalar.activation(hh[u % 2][:, :], h32[u % 2][:, :], ACT.Copy).then_inc(hh_ready, 1)

        def ffn_hl(dve, u):
            dve.wait_ge(hh_ready, u + 1)
            nc.vector.tensor_tensor(hl[u % 2][:, :], h32[u % 2][:, :], hh[u % 2][:, :],
                                    ALU.subtract).then_inc(hl_ready, 1)

        def sum_drive(n, half):
            row, c = divmod(n, KT)
            steps = slice(half * HS, (half + 1) * HS)
            nc.scalar.activation(sum_r[:, steps, row, c, :], dr[:, steps, c, :], ACT.Identity,
                                 bias=constant[:, row, c:c + 1],
                                 scale=float(LINEAR[row, BY_R] * S)).then_inc(sum_r_ready, 1)

        def hist_high(act, c):
            nc.scalar.activation(xh[:, c, :], hist[:, c].rearrange("p t b -> p (t b)"), ACT.Copy,
                                 scale=1.0 / S).then_inc(xh_ready, 1)

        def hist_low(dve, c):
            dve.wait_ge(xh_ready, c + 1)
            nc.vector.scalar_tensor_tensor(xl[:, c, :], hist[:, c].rearrange("p t b -> p (t b)"), 1.0 / S,
                                           xh[:, c, :], ALU.mult, ALU.subtract).then_inc(xl_ready, 1)

        def norm_sum(act):
            act.wait_ge(down_done, UNITS)
            nc.scalar.activation(junk[:, :], y_ps[:, :], ACT.Square,
                                 accum_out=sumsq[:, 0:1]).then_inc(sumsq_ready, 1)

        def norm_root(pool):
            pool.wait_ge(sumsq_ready, 1)
            nc.gpsimd.tensor_scalar(meansq[:, :], sumsq[:, :], 1.0 / N, EPS * Y_SCALE * Y_SCALE,
                                    ALU.mult, ALU.add).then_inc(rinv_ready, 1)
            pool.wait_ge(rinv_ready, 1)
            nc.gpsimd.tensor_tensor(rinv[:, :], meansq[:, :], mhalf[:, :], ALU.pow).then_inc(rinv_ready, 1)

        def norm_out(dve, n):
            if n == 0:
                dve.wait_ge(rinv_ready, 2)
                dve.wait_ge(xres_in, 16)
                dve.wait_ge(osb_free, 1)
            c = slice(n * P, (n + 1) * P)
            nc.vector.scalar_tensor_tensor(osb[:, c], y_ps[:, c], rinv[:, 0:1], xres[:, c],
                                           ALU.mult, ALU.add).then_inc(out_ready, 1)

        def sp_residual(sp, k):
            sp.wait_ge(stored, 16)
            sp.sem_inc(stored, -16)
            sp.sem_inc(osb_free, 1)
            sp.dma_start(xres[:, :], x_rows(x, k)).then_inc(xres_in, 16)

        def sp_store(sp, k):
            sp.wait_ge(out_ready, KT)
            sp.dma_start(x_rows(out, k), osb[:, :]).then_inc(stored, 16)

        def x_rows(ap, k):
            return ap.rearrange("b (k t) n -> k t b n", t=STEPS)[k]

        with nc.Block() as block:
            @block.sync
            def _(sp):
                sp.dma_start(coup[:, :, :], coupling_t).then_inc(scan_in, 16)
                sp.dma_start(q_raw[:, :, :], cond_t).then_inc(scan_in, 16)
                sp.dma_start(bias[:, :], bias_t).then_inc(scan_in, 16)
                for half in range(2):
                    sp.dma_start(dr[:, half * HS:(half + 1) * HS], drive[half]).then_inc(loaded, 16)
                for u in range(UNITS):
                    if u >= 2:
                        sp.wait_ge(dq_lo, u - 1)
                    words = packed[u].unsqueeze(1)
                    sp.dma_start(raw[u % 2][:, :], words.to_broadcast([P // 8, 8, UW])).then_inc(raw_in[u % 2], 16)
                    sp.dma_start(sc[u % 2][:, :], scales[u:u + 1, :].to_broadcast([P, UW])).then_inc(raw_in[u % 2], 16)
                sp.wait_ge(loaded, 32)

            @block.gpsimd
            def _(pool):
                nc.gpsimd.iota(shift[:, :], [[0, 1]], base=0, channel_multiplier=1).then_inc(pool_link, 1)
                for name, column in (("p", BY_P), ("q1", BY_Q1), ("q2", BY_Q2), ("q3", BY_Q3)):
                    for row in range(1, ROWS):
                        nc.gpsimd.memset(by[name][:, row], float(LINEAR[row, column]))
                nc.gpsimd.memset(mhalf[:, :], -0.5)

            @block.scalar
            def _(act):
                nc.scalar.preload_act_table(ACT.Silu)
                act.wait_ge(scan_in, 48)
                for n, coef in enumerate(COEF):
                    nc.scalar.activation(wscan[:, n, 0], coup[:, :, :], ACT.Copy,
                                         scale=coef * S).then_inc(tanh_hi, 1)
                act.wait_ge(loaded, 32)
                act.wait_ge(dve_link, ROWS)
                for n in range(SUM_R_PARTS):
                    sum_drive(n, 0)
                for u in range(UNITS):
                    act.wait_ge(dq_w32, u + 1)
                    nc.scalar.activation(wffn[:, u, 0, :], w32[:, :], ACT.Copy).then_inc(dq_hi, 1)

            @block.vector
            def _(dve):
                count = [0]

                def link(ins):
                    count[0] += 1
                    ins.then_inc(dve_link, 1)
                    dve.wait_ge(dve_link, count[0])

                dve.wait_ge(scan_in, 48)
                nc.vector.tensor_scalar(p_state[:, :, :], q_raw[:, :, :], S, None, ALU.mult)
                nc.vector.tensor_scalar(hist[:, :, STEPS - 1, :], q_raw[:, :, :], S, None, ALU.mult)
                for row in range(ROWS):
                    link(nc.vector.tensor_scalar(constant[:, row], bias[:, :], float(LINEAR[row, BY_R] * S),
                                                 float(LINEAR[row, BY_ONE] * S), ALU.mult, ALU.add))
                for c in range(KT):
                    wide = constant[:, ROWS - 1, c:c + 1].unsqueeze(2).to_broadcast([P, STEPS, B])
                    nc.vector.tensor_copy(sum_r[:, :, ROWS - 1, c, :], wide)
                dve.wait_ge(pool_link, 1)
                link(nc.vector.tensor_scalar(shift[:, :], shift[:, :], 7, 2, ALU.bitwise_and,
                                             ALU.logical_shift_left))
                link(nc.vector.tensor_copy(q_raw[:, :, :], hist[:, :, STEPS - 1, :]))
                for n, coef in enumerate(COEF):
                    dve.wait_ge(tanh_hi, n + 1)
                    nc.vector.scalar_tensor_tensor(wscan[:, n, 1], coup[:, :, :], coef * S, wscan[:, n, 0],
                                                   ALU.mult, ALU.subtract)
                for u in range(UNITS):
                    dve.wait_ge(raw_in[u % 2], 32 * (u // 2 + 1))
                    link(nc.vector.tensor_scalar(nib[:, :], raw[u % 2][:, :], shift[:, 0:1], 15,
                                                 ALU.logical_shift_right, ALU.bitwise_and))
                    link(nc.vector.scalar_tensor_tensor(nib2[:, :], nib[:, :], 3, nib[:, :],
                                                        ALU.logical_shift_left, ALU.bitwise_or))
                    link(nc.vector.tensor_scalar(nib[:, :], nib2[:, :], 0x47, 9, ALU.bitwise_and,
                                                 ALU.logical_shift_left))
                    fp4 = nib[:, :].bitcast(F16).rearrange("p (n two) -> p n two", two=2)[:, :, 0]
                    nc.vector.scalar_tensor_tensor(w32[:, :], fp4, FP4_BITS * W_SCALE, sc[u % 2][:, :],
                                                   ALU.mult, ALU.mult).then_inc(dq_w32, 1)
                    dve.wait_ge(dq_hi, u + 1)
                    nc.vector.tensor_tensor(wffn[:, u, 1, :], w32[:, :], wffn[:, u, 0, :],
                                            ALU.subtract).then_inc(dq_lo, 1)
                    dve.wait_ge(dq_lo, u + 1)
        end_of_block()

        def time_block(k, ffn):
            with nc.Block() as block:
                @block.sync
                def _(sp):
                    sp.dma_start(dr[:, 0:HS], drive[2 * k + 2]).then_inc(drive_lo, 16)
                    if ffn:
                        sp_residual(sp, k - 1)
                    sp.wait_ge(sum_r_ready, SUM_R_PARTS)
                    sp.dma_start(dr[:, HS:STEPS], drive[2 * k + 3]).then_inc(drive_hi, 16)
                    sp.wait_ge(drive_hi, 16)
                    if ffn:
                        sp_store(sp, k - 1)

                @block.tensor
                def _(pe):
                    def couple(s, part, k_half, n_half):
                        w, t_in = STAGE_COEF[s % 4], th[s % 2]
                        for c in range(HC):
                            for kt in range(k_half * HC, (k_half + 1) * HC):
                                cols = slice((n_half * HC + c) * P, (n_half * HC + c + 1) * P)
                                to = prod[n_half][:, :, c * B:(c + 1) * B]
                                first = part == 1 and k_half == 0 and c == 0 and kt == 0
                                last = part == 0 and k_half == 1 and c == HC - 1 and kt == KT - 1
                                i = nc.tensor.matmul(to[:, 0] if part else to, wscan[:, w, part, kt, cols],
                                                     t_in[:, kt, 0, :] if part else t_in[:, kt, :, :],
                                                     start=first, stop=last, skip_group_check=True)
                        return i

                    for s in range(STAGES):
                        pe.wait_ge(tanh_hi, 2 * s + 1)
                        couple(s, 1, 0, 0)
                        if s:
                            pe.wait_ge(q_ready, 2 * s)
                        couple(s, 1, 0, 1)
                        pe.wait_ge(tanh_hi, 2 * s + 2)
                        couple(s, 1, 1, 0)
                        couple(s, 1, 1, 1)
                        pe.wait_ge(tanh_lo, 2 * s + 1)
                        couple(s, 0, 0, 0)
                        pe.wait_ge(tanh_lo, 2 * s + 2)
                        couple(s, 0, 1, 0).then_inc(products, 1)
                        couple(s, 0, 0, 1)
                        couple(s, 0, 1, 1).then_inc(products, 1)
                        if ffn:
                            for n, (kind, u, j) in enumerate(PE_AT[s]):
                                if kind == "gate_up" and u == 0 and j == 0:
                                    pe.wait_ge(xl_ready, KT)
                                (gate_up if kind == "gate_up" else down)(pe, u, j)

                @block.scalar
                def _(act):
                    for s in range(STAGES):
                        q = q_raw if s % 4 == 0 else q_stage[s % 4 - 1]
                        for half in range(2):
                            c = slice(half * HC, (half + 1) * HC)
                            if s:
                                act.wait_ge(q_ready, 2 * s - 1 + half)
                            nc.scalar.activation(th[s % 2][:, c, 0, :], q[:, c, :], ACT.Tanh,
                                                 scale=1.0 / S).then_inc(tanh_hi, 1)
                            nc.scalar.activation(t32[:, c, :], q[:, c, :], ACT.Tanh,
                                                 scale=1.0 / S).then_inc(tanh_32, 1)
                        if s % 2 == 1 and s // 2 < SUM_R_PARTS:
                            sum_drive(s // 2, 1)
                        if s == 2 * SUM_R_PARTS + 1:
                            act.wait_ge(drive_lo, 16)
                        if s % 2 == 1 and s // 2 >= SUM_R_PARTS:
                            sum_drive(s // 2 - SUM_R_PARTS, 0)
                        if ffn:
                            if s < KT:
                                hist_high(act, s)
                            for u in range(UNITS):
                                if s == GATE_UP_AT[u] + 1:
                                    ffn_silu(act, u)
                                if s == GATE_UP_AT[u] + 3:
                                    ffn_hh(act, u)
                            if s == LAST_DOWN + 1:
                                norm_sum(act)

                @block.vector
                def _(dve):
                    linear = [linear0[:, :, :], sum_q1[:, 1], sum_q2[:, 2], sum_q3[:, 3]]
                    for s in range(STAGES):
                        t, i = divmod(s, 4)
                        before = hist[:, :, (t - 1) % STEPS, :]
                        q = before if i == 0 else q_stage[i - 1][:, :, :]
                        q_next = q_raw if i == 3 else q_stage[i]
                        def square():
                            if i == 0 and t:
                                dve.wait_ge(clipped, t)
                            elif s:
                                dve.wait_ge(q_ready, 2 * s)
                            nc.vector.tensor_tensor(q_sq[:, :, :], q, q, ALU.mult).then_inc(squared, 1)

                        def cube():
                            dve.wait_ge(squared, s + 1)
                            nc.vector.scalar_tensor_tensor(q_cub[:, :, :], q_sq[:, :, :], SHIFT[i], q,
                                                           ALU.add, ALU.mult).then_inc(cubed, 1)

                        def low_part(half):
                            c = slice(half * HC, (half + 1) * HC)
                            dve.wait_ge(tanh_32, 2 * s + 1 + half)
                            nc.vector.tensor_tensor(th[s % 2][:, c, 1, :], t32[:, c, :], th[s % 2][:, c, 0, :],
                                                    ALU.subtract).then_inc(tanh_lo, 1)

                        if i:
                            square()
                            low_part(0)
                            cube()
                            low_part(1)
                        else:
                            low_part(0)
                            square()
                            low_part(1)
                            cube()
                        if i == 0:
                            if t == HS:
                                dve.wait_ge(sum_r_ready, SUM_R_PARTS)
                            if t:
                                dve.wait_ge(p_ready, t)
                            nc.vector.scalar_tensor_tensor(linear0[:, :, :], p_state[:, :, :],
                                                           float(LINEAR[0, BY_P]), sum_r[:, t, 0], ALU.mult,
                                                           ALU.add).then_inc(dve_link, 1)
                            dve.wait_ge(dve_link, 2 * t + 1)
                        dve.wait_ge(cubed, s + 1)
                        if i:
                            dve.wait_ge(pool_local, 3 * t + i)
                        nc.vector.scalar_tensor_tensor(local_ps, halves(q_cub[:, :, :]), CUBE[i], halves(linear[i]),
                                                       ALU.mult, ALU.add).then_inc(local_in, 1)
                        if i == 3:
                            nc.vector.scalar_tensor_tensor(p_sum[:, :, :], q, float(LINEAR[4, BY_Q4]),
                                                           sum_q3[:, 4], ALU.mult, ALU.add).then_inc(dve_link, 1)
                            dve.wait_ge(dve_link, 2 * t + 2)
                            nc.vector.tensor_scalar(p_state[:, :, :], p_sum[:, :, :], -CLAMP * S, CLAMP * S,
                                                    ALU.max, ALU.min).then_inc(p_ready, 1)
                        if ffn:
                            if s < KT:
                                hist_low(dve, s)
                            for u in range(UNITS):
                                if s == GATE_UP_AT[u] + 2:
                                    ffn_h32(dve, u)
                                if s == GATE_UP_AT[u] + 4:
                                    ffn_hl(dve, u)
                            if LAST_DOWN + 3 <= s < LAST_DOWN + 3 + KT:
                                norm_out(dve, s - LAST_DOWN - 3)
                        for half in range(2):
                            dve.wait_ge(products, 2 * s + 1 + half)
                            if half == 0:
                                dve.wait_ge(local_in, s + 1)
                            nc.vector.tensor_reduce(q_next[:, half * HC:(half + 1) * HC, :], three[half], AX.X,
                                                    ALU.add).then_inc(q_ready, 1)
                        if i == 3:
                            dve.wait_ge(q_ready, 2 * s + 2)
                            if ffn and t == 0:
                                dve.wait_ge(xl_ready, KT)
                            nc.vector.tensor_scalar(hist[:, :, t, :], q_raw[:, :, :], -CLAMP * S, CLAMP * S,
                                                    ALU.max, ALU.min).then_inc(clipped, 1)

                @block.gpsimd
                def _(pool):
                    count = [0]

                    def link(ins):
                        count[0] += 1
                        ins.then_inc(pool_link, 1)
                        pool.wait_ge(pool_link, count[0])

                    def add_times(to, x, name, base, first, signal=link):
                        rows = slice(first, ROWS)
                        wide = x.unsqueeze(1).to_broadcast([P, ROWS - first, KT, B])
                        link(nc.gpsimd.tensor_tensor(term[:, rows], wide, by[name][:, rows], ALU.mult))
                        signal(nc.gpsimd.tensor_tensor(to[:, rows], term[:, rows], base[:, rows], ALU.add))

                    def to_dve(ins):
                        ins.then_inc(pool_local, 1)
                        locals_done[0] += 1
                        pool.wait_ge(pool_local, locals_done[0])

                    locals_done = [0]
                    for t in range(STEPS):
                        if t == HS:
                            pool.wait_ge(sum_r_ready, SUM_R_PARTS)
                        if t:
                            pool.wait_ge(p_ready, t)
                        add_times(sum_p, p_state[:, :, :], "p", sum_r[:, t], 1, link)
                        if t:
                            pool.wait_ge(clipped, t)
                        add_times(sum_q1, hist[:, :, (t - 1) % STEPS, :], "q1", sum_p, 1, to_dve)
                        pool.wait_ge(q_ready, 8 * t + 2)
                        add_times(sum_q2, q_stage[0][:, :, :], "q2", sum_q1, 2, to_dve)
                        pool.wait_ge(q_ready, 8 * t + 4)
                        add_times(sum_q3, q_stage[1][:, :, :], "q3", sum_q2, 3, to_dve)
                        if ffn and t == (LAST_DOWN + 1) // 4:
                            norm_root(pool)
            end_of_block()

        time_block(0, ffn=False)
        with nc.Block() as block:
            @block.sync
            def _(sp):
                sp.sem_inc(stored, 16)
        with nc.Fori(1, BLOCKS) as k:
            time_block(k, ffn=True)

        with nc.Block() as block:
            @block.sync
            def _(sp):
                sp_residual(sp, BLOCKS - 1)
                sp_store(sp, BLOCKS - 1)
                sp.wait_ge(stored, 16)

            @block.tensor
            def _(pe):
                pe.wait_ge(xl_ready, KT)
                for u in range(UNITS + 1):
                    if u < UNITS:
                        for j in range(2 * GU_PARTS * KT):
                            gate_up(pe, u, j)
                    if u >= 1:
                        for j in range(2 * DOWN_PARTS):
                            down(pe, u - 1, j)

            @block.scalar
            def _(act):
                for c in range(KT):
                    hist_high(act, c)
                for u in range(UNITS):
                    ffn_silu(act, u)
                    ffn_hh(act, u)
                norm_sum(act)

            @block.vector
            def _(dve):
                for c in range(KT):
                    hist_low(dve, c)
                for u in range(UNITS):
                    ffn_h32(dve, u)
                    ffn_hl(dve, u)
                for n in range(KT):
                    norm_out(dve, n)

            @block.gpsimd
            def _(pool):
                norm_root(pool)


def kernel(x, cond_2048, L0_cond_coupling, L0_cond_bias, L0_ffn_gate_up_packed, L0_ffn_gate_up_scales,
           L0_ffn_down_packed, L0_ffn_down_scales):
    import concourse.bacc as bacc
    from concourse.bass_utils import run_bass_kernel_spmd

    x = np.asarray(x)
    halves = 2 * BLOCKS
    drive = x.reshape(B, halves, T // halves, KT, P).transpose(1, 4, 2, 3, 0)
    drive = np.concatenate([drive, drive[-2:]])
    gu = np.asarray(L0_ffn_gate_up_packed).reshape(2, UNITS, P, KT, P // 8).transpose(1, 4, 0, 3, 2)
    dn = np.asarray(L0_ffn_down_packed).reshape(N, UNITS, P // 8).transpose(1, 2, 0)
    packed = np.concatenate([gu.reshape(UNITS, P // 8, 2 * KT * P), dn], axis=2)
    gus = np.asarray(L0_ffn_gate_up_scales).reshape(KT, 2, UNITS, P).transpose(2, 1, 0, 3)
    scales = np.concatenate([gus.reshape(UNITS, 2 * KT * P), np.asarray(L0_ffn_down_scales)], axis=1)
    arrays = {
        "x": x,
        "drive": drive,
        "cond_t": np.asarray(cond_2048).reshape(B, KT, P).transpose(2, 1, 0),
        "coupling_t": np.asarray(L0_cond_coupling).reshape(N, KT, P).transpose(2, 1, 0),
        "bias_t": np.asarray(L0_cond_bias).reshape(KT, P).T,
        "packed": packed,
        "scales": scales,
    }
    arrays = {name: np.ascontiguousarray(a) for name, a in arrays.items()}
    nc = bacc.Bacc("TRN2", target_bir_lowering=False, num_devices=1)
    args = [nc.dram_tensor(name, a.shape, mybir.dt.from_np(a.dtype), kind="ExternalInput").ap()
            for name, a in arrays.items()]
    out = nc.dram_tensor("out", (B, T, N), F32, kind="ExternalOutput").ap()
    program(nc, *args, out)
    r = run_bass_kernel_spmd(nc, [arrays], core_ids=[0])
    return r.results[0]["out"]
```

```python
from contextlib import ExitStack

import numpy as np

import concourse.bass as bass
from concourse import mybir

F32 = mybir.dt.float32
F16 = mybir.dt.float16
I32 = mybir.dt.int32
ALU = mybir.AluOpType
ACT = mybir.ActivationFunctionType
AX = mybir.AxisListType

B, T, N = 8, 256, 512
I = 1408
P = 128
KT = N // P
HC = KT // 2
HB = HC * B
STEPS = 16
BLOCKS = T // STEPS
STAGES = 4 * STEPS
HS = STEPS // 2
TOK = STEPS * B
UNITS = I // P
UW = 2 * KT * P + N

DT, EPSILON, ALPHA, BETA, CLAMP = 0.01, 0.08, 0.7, 0.8, 20.0
S = 65536.0
CH = DT / 2
AH = CH * EPSILON
COEF = [CH, 2 * CH, CH / 3]
STAGE_COEF = [0, 0, 1, 2]


def linear_parts():
    r, p, q1, q2, q3, q4, one = np.eye(7)
    a, b = AH, BETA
    p2 = p + a * (q1 + ALPHA * one - b * p)
    p3 = p + a * (q2 + ALPHA * one - b * p2)
    p4 = p + 2 * a * (q3 + ALPHA * one - b * p3)
    p_next = (-p + p2 + 2 * p3 + p4 + a * (q4 + ALPHA * one - b * p4)) / 3
    return np.stack([q1 + CH * (r - p), q1 + CH * (r - p2), q1 + 2 * CH * (r - p3),
                     (-q1 + q2 + 2 * q3 + q4 + CH * (r - p4)) / 3, p_next])


LINEAR = linear_parts()
ROWS = len(LINEAR)
SUM_R_PARTS = (ROWS - 1) * KT
BY_R, BY_P, BY_Q1, BY_Q2, BY_Q3, BY_Q4, BY_ONE = range(7)
CUBE = [-COEF[STAGE_COEF[i]] / (3 * S * S) for i in range(4)]
SHIFT = [(COEF[STAGE_COEF[i]] + LINEAR[i, BY_Q1 + i]) / CUBE[i] for i in range(4)]

W_SCALE = 64.0
H_SCALE = 2.0 ** -9
Y_SCALE = W_SCALE * H_SCALE
UNPACK_BUFS = 3
FP4_BITS = 2.0 ** 14
EPS = 1e-6

FFN_FIRST = 2
GU_PARTS = 4
DOWN_PARTS = 4
DOWN_LAG = 5
START_LATE = 4
CATCH_UP = 6


def ffn_schedule(late, catch_up):
    gate_ups = [(u, j) for u in range(UNITS) for j in range(2 * GU_PARTS * KT)]
    downs = [(u, j) for u in range(UNITS) for j in range(2 * DOWN_PARTS)]
    down_cost = N // 2 // P
    even = (len(gate_ups) + down_cost * (len(downs) - 2 * DOWN_PARTS)) / STAGES
    at, done, budget, s = {}, {}, 0.0, FFN_FIRST
    while gate_ups or downs:
        if s >= FFN_FIRST + late + catch_up:
            budget += even
        elif s >= FFN_FIRST + late:
            budget += even * (late + catch_up) / catch_up
        while gate_ups or downs:
            down_now = downs and s >= done.get(downs[0][0], s) + DOWN_LAG
            if not (down_now or gate_ups) or budget < (down_cost if down_now else 1):
                break
            u, j = (downs if down_now else gate_ups).pop(0)
            at.setdefault(s, []).append(("down" if down_now else "gate_up", u, j))
            budget -= down_cost if down_now else 1
            if not down_now and j == 2 * GU_PARTS * KT - 1:
                done[u] = s
        s += 1
    return at, done


class Schedule:

    def __init__(self, late, catch_up):
        self.pe, gate_up = ffn_schedule(late, catch_up)
        self.silu = {s + 1: u for u, s in gate_up.items()}
        self.h32 = {s + 2: u for u, s in gate_up.items()}
        self.hh = {s + 3: u for u, s in gate_up.items()}
        self.hl = {s + 4: u for u, s in gate_up.items()}
        self.norm_sum = max(self.pe) + 1
        self.norm_root = self.norm_sum + 1
        busy = set(self.h32) | set(self.hl) | {s + STAGES for s in (*self.h32, *self.hl)}
        free = [s for s in range(self.norm_sum + 3, 2 * STAGES) if s not in busy]
        self.norm_out = {s: n for n, s in enumerate(free[:KT])}
        self.end = max(self.norm_out) + 1

    def rest(self):
        return [{s: x for s, x in part.items() if s >= STAGES} for part in
                (self.pe, self.silu, self.h32, self.hh, self.hl)] + [self.norm_sum]


SCHEDULE = Schedule(0, 0)
FIRST_SCHEDULE = Schedule(START_LATE, CATCH_UP)
assert FIRST_SCHEDULE.rest() == SCHEDULE.rest()
assert UNITS % 2 == 1


class Signals:

    def __init__(self, new, tag, parity):
        self.parity = parity
        made = []

        def sem(name):
            made.append(new(f"{name}_{tag}"))
            return made[-1]

        self.q_ready = sem("q_ready")
        self.tanh_hi = sem("tanh_hi")
        self.tanh_32 = sem("tanh_32")
        self.tanh_lo = sem("tanh_lo")
        self.products = sem("products")
        self.squared = sem("squared")
        self.cubed = sem("cubed")
        self.local_in = sem("local_in")
        self.clipped = sem("clipped")
        self.linear0 = sem("linear0")
        self.pool_local = sem("pool_local")
        self.pool_link = sem("pool_link")
        self.p_ready = sem("p_ready")
        self.sum_r_ready = sem("sum_r_ready")
        self.drive_lo = sem("drive_lo")
        self.drive_hi = sem("drive_hi")
        self.xh_ready = sem("xh_ready")
        self.xl_ready = sem("xl_ready")
        self.gu_ready = sem("gu_ready")
        self.silu_ready = sem("silu_ready")
        self.h32_ready = sem("h32_ready")
        self.hh_ready = sem("hh_ready")
        self.hl_ready = sem("hl_ready")
        self.down_done = sem("down_done")
        self.sumsq_ready = sem("sumsq_ready")
        self.rinv_ready = sem("rinv_ready")
        self.out_ready = sem("out_ready")
        self.xres_in = sem("xres_in")
        self.osb_free = sem("osb_free")
        self.range = range(made[0].num, made[-1].num + 1)
        assert len(self.range) == len(made)


def program(nc, x, drive, cond_t, coupling_t, bias_t, packed, scales, out):
    ctx = ExitStack()

    def sb(name, shape, dt=F32):
        return ctx.enter_context(nc.sbuf_tensor(name, shape, dt))

    def sem(name):
        return ctx.enter_context(nc.semaphore(name))

    with ctx:
        coup = sb("coup", [P, KT, N])
        wscan = sb("wscan", [P, 3, 2, KT, N], F16)
        hist = sb("hist", [P, KT, STEPS, B])
        q_raw = sb("q_raw", [P, KT, B])
        q_stage = [sb(f"q_stage{i}", [P, KT, B]) for i in (2, 3, 4)]
        p_state = sb("p_state", [P, KT, B])
        p_term = sb("p_term", [P, KT, B])
        p_sum = sb("p_sum", [P, KT, B])
        th = [sb(f"th{i}", [P, KT, 2, B], F16) for i in range(2)]
        t32 = sb("t32", [P, KT, B])
        q_sq = sb("q_sq", [P, KT, B])
        q_cub = sb("q_cub", [P, KT, B])
        by = {n: sb(f"by_{n}", [P, ROWS, KT, B]) for n in ("p", "q1", "q2", "q3")}
        constant = sb("constant", [P, ROWS, KT])
        term = sb("term", [P, ROWS, KT, B])
        sum_r = sb("sum_r", [P, STEPS, ROWS, KT, B])
        linear0 = sb("linear0", [P, KT, B])
        sum_p = sb("sum_p", [P, ROWS, KT, B])
        sum_q1 = sb("sum_q1", [P, ROWS, KT, B])
        sum_q2 = sb("sum_q2", [P, ROWS, KT, B])
        sum_q3 = sb("sum_q3", [P, ROWS, KT, B])
        bias = sb("bias", [P, KT])
        dr = sb("dr", [P, STEPS, KT, B])
        wffn = sb("wffn", [P, UNITS, 2, UW], F16)
        raw = [sb(f"raw{i}", [P, UW], I32) for i in range(UNPACK_BUFS)]
        sc = [sb(f"sc{i}", [P, UW], F16) for i in range(UNPACK_BUFS)]
        nib = [sb(f"nib{i}", [P, UW], I32) for i in range(2)]
        w32 = [sb(f"w32_{i}", [P, UW]) for i in range(UNPACK_BUFS)]
        shift = sb("shift", [P, 1], I32)
        xh = [sb(f"xh{i}", [P, KT, TOK], F16) for i in range(2)]
        xl = [sb(f"xl{i}", [P, KT, TOK], F16) for i in range(2)]
        silu = [sb(f"silu{i}", [P, TOK]) for i in range(2)]
        h32 = [sb(f"h32_{i}", [P, TOK]) for i in range(2)]
        hh = [sb(f"hh{i}", [P, TOK], F16) for i in range(2)]
        hl = [sb(f"hl{i}", [P, TOK], F16) for i in range(2)]
        junk = sb("junk", [P, N])
        sumsq = sb("sumsq", [P, 1])
        meansq = sb("meansq", [P, 1])
        rinv = sb("rinv", [P, 1])
        mhalf = sb("mhalf", [P, 1])
        xres = sb("xres", [P, N])
        osb = sb("osb", [P, N])

        APART = 256
        scan_ps = ctx.enter_context(nc.psum_tensor("scan_ps", [P, 6 * APART], F32))
        gu_ps = [ctx.enter_context(nc.psum_tensor(f"gu_ps{i}", [P, 512], F32)) for i in range(2)]
        y_ps = [ctx.enter_context(nc.psum_tensor(f"y_ps{i}", [P, N], F32)) for i in range(2)]
        prod, three = [], []
        for half in range(2):
            own = scan_ps[:, half * 3 * APART:(half + 1) * 3 * APART].rearrange("p (k r) -> p k r", k=3)[:, :, 0:HB]
            prod.append(own[:, half:half + 2])
            three.append(own.rearrange("p k (c b) -> p c b k", b=B))
        local_ps = scan_ps[:, 2 * APART:4 * APART].rearrange("p (h r) -> p h r", h=2)[:, :, 0:HB]

        def halves(tile):
            return tile.rearrange("p (h c) b -> p h (c b)", h=2)

        scan_in = sem("scan_in")
        loaded = sem("loaded")
        coup_in = sem("coup_in")
        raw_in = [sem(f"raw_in{i}") for i in range(UNPACK_BUFS)]
        iota_done = sem("iota_done")
        setup_link = sem("setup_link")
        constants = sem("constants")
        coup_hi = sem("coup_hi")
        sums_set = sem("sums_set")
        dq_w32 = sem("dq_w32")
        dq_hi = sem("dq_hi")
        dq_lo = sem("dq_lo")
        stored = sem("stored")
        signals = [Signals(sem, "even", 0), Signals(sem, "odd", 1)]

        def wait_unit(engine, name, f, g, u):
            if u >= 2:
                engine.wait_ge(name(f), u - 1)
            elif g:
                engine.wait_ge(name(g), UNITS - 1 + u)

        def gate_up(pe, f, g, u, j):
            b = (u + f.parity) % 2
            half, r = divmod(j, GU_PARTS * KT)
            kt, which = divmod(r, GU_PARTS)
            part, tokens = ((0, xh), (0, xl), (1, xh), (1, xl))[which]
            col = (half * KT + kt) * P
            if j == 0:
                wait_unit(pe, lambda s: s.h32_ready, f, g, u)
            if u == 0 and half == 0 and which == 0:
                pe.wait_ge(f.xl_ready, kt + 1)
            i = nc.tensor.matmul(gu_ps[b][:, half * P:(half + 1) * P], wffn[:, u, part, col:col + P],
                                 tokens[f.parity][:, kt, :], start=(r == 0), stop=(r == GU_PARTS * KT - 1))
            if j == 2 * GU_PARTS * KT - 1:
                i.then_inc(f.gu_ready, 1)

        def down(pe, f, u, j):
            b = (u + f.parity) % 2
            if j == 0:
                pe.wait_ge(f.hl_ready, u + 1)
            which, half = divmod(j, 2)
            part, h = ((0, hh), (0, hl), (1, hh), (1, hl))[which]
            cols = slice(half * N // 2, (half + 1) * N // 2)
            i = nc.tensor.matmul(y_ps[f.parity][:, cols], h[b][:, :], wffn[:, u, part, 2 * KT * P:][:, cols],
                                 start=(u == 0 and j == 0), stop=(u == UNITS - 1 and which == DOWN_PARTS - 1),
                                 skip_group_check=True)
            if j == 2 * DOWN_PARTS - 1:
                i.then_inc(f.down_done, 1)

        def ffn_silu(act, f, g, u):
            b = (u + f.parity) % 2
            act.wait_ge(f.gu_ready, u + 1)
            wait_unit(act, lambda s: s.h32_ready, f, g, u)
            nc.scalar.activation(silu[b][:, :], gu_ps[b][:, 0:P], ACT.Silu,
                                 scale=1.0 / W_SCALE).then_inc(f.silu_ready, 1)

        def ffn_h32(dve, f, g, u):
            b = (u + f.parity) % 2
            dve.wait_ge(f.silu_ready, u + 1)
            wait_unit(dve, lambda s: s.hl_ready, f, g, u)
            nc.vector.scalar_tensor_tensor(h32[b][:, :], gu_ps[b][:, P:2 * P], H_SCALE / W_SCALE,
                                           silu[b][:, :], ALU.mult, ALU.mult).then_inc(f.h32_ready, 1)

        def ffn_hh(act, f, g, u):
            b = (u + f.parity) % 2
            act.wait_ge(f.h32_ready, u + 1)
            wait_unit(act, lambda s: s.down_done, f, g, u)
            nc.scalar.activation(hh[b][:, :], h32[b][:, :], ACT.Copy).then_inc(f.hh_ready, 1)

        def ffn_hl(dve, f, u):
            b = (u + f.parity) % 2
            dve.wait_ge(f.hh_ready, u + 1)
            nc.vector.tensor_tensor(hl[b][:, :], h32[b][:, :], hh[b][:, :], ALU.subtract).then_inc(f.hl_ready, 1)

        def hist_high(act, f, c):
            nc.scalar.activation(xh[f.parity][:, c, :], hist[:, c].rearrange("p t b -> p (t b)"), ACT.Copy,
                                 scale=1.0 / S).then_inc(f.xh_ready, 1)

        def hist_low(dve, f, c):
            dve.wait_ge(f.xh_ready, c + 1)
            nc.vector.scalar_tensor_tensor(xl[f.parity][:, c, :], hist[:, c].rearrange("p t b -> p (t b)"), 1.0 / S,
                                           xh[f.parity][:, c, :], ALU.mult, ALU.subtract).then_inc(f.xl_ready, 1)

        def norm_sum(act, f):
            act.wait_ge(f.down_done, UNITS)
            nc.scalar.activation(junk[:, :], y_ps[f.parity][:, :], ACT.Square,
                                 accum_out=sumsq[:, 0:1]).then_inc(f.sumsq_ready, 1)

        def norm_root(pool, f):
            pool.wait_ge(f.sumsq_ready, 1)
            nc.gpsimd.tensor_scalar(meansq[:, :], sumsq[:, :], 1.0 / N, EPS * Y_SCALE * Y_SCALE,
                                    ALU.mult, ALU.add).then_inc(f.rinv_ready, 1)
            pool.wait_ge(f.rinv_ready, 1)
            nc.gpsimd.tensor_tensor(rinv[:, :], meansq[:, :], mhalf[:, :], ALU.pow).then_inc(f.rinv_ready, 1)

        def norm_out(dve, f, n):
            if n == 0:
                dve.wait_ge(f.rinv_ready, 2)
                dve.wait_ge(f.xres_in, 16)
                dve.wait_ge(f.osb_free, 1)
            c = slice(n * P, (n + 1) * P)
            nc.vector.scalar_tensor_tensor(osb[:, c], y_ps[f.parity][:, c], rinv[:, 0:1], xres[:, c],
                                           ALU.mult, ALU.add).then_inc(f.out_ready, 1)

        def act_ffn(act, plan, f, g, s):
            if s in plan.silu:
                ffn_silu(act, f, g, plan.silu[s])
            if s in plan.hh:
                ffn_hh(act, f, g, plan.hh[s])
            if s == plan.norm_sum:
                norm_sum(act, f)

        def dve_ffn(dve, plan, f, g, s):
            if s in plan.h32:
                ffn_h32(dve, f, g, plan.h32[s])
            if s in plan.hl:
                ffn_hl(dve, f, plan.hl[s])
            if s in plan.norm_out:
                norm_out(dve, f, plan.norm_out[s])

        def pe_ffn(pe, plan, f, g, s):
            for kind, u, j in plan.pe.get(s, []):
                if kind == "gate_up":
                    gate_up(pe, f, g, u, j)
                else:
                    down(pe, f, u, j)

        def sum_drive(n, half, done):
            row, c = divmod(n, KT)
            steps = slice(half * HS, (half + 1) * HS)
            nc.scalar.activation(sum_r[:, steps, row, c, :], dr[:, steps, c, :], ACT.Identity,
                                 bias=constant[:, row, c:c + 1],
                                 scale=float(LINEAR[row, BY_R] * S)).then_inc(done, 1)

        def sp_store(sp, f, k):
            sp.wait_ge(f.out_ready, KT)
            sp.dma_start(x_rows(out, k), osb[:, :]).then_inc(stored, 16)
            sp.wait_ge(stored, 16)
            sp.sem_inc(stored, -16)

        def sp_residual(sp, f, k):
            sp.sem_inc(f.osb_free, 1)
            sp.dma_start(xres[:, :], x_rows(x, k)).then_inc(f.xres_in, 16)

        def x_rows(ap, k):
            return ap.rearrange("b (k t) n -> k t b n", t=STEPS)[k]

        with nc.Block() as block:
            @block.sync
            def _(sp):
                def load_unit(u):
                    b = u % UNPACK_BUFS
                    if u >= UNPACK_BUFS:
                        sp.wait_ge(dq_w32, u - UNPACK_BUFS + 1)
                    words = packed[u].unsqueeze(1)
                    sp.dma_start(raw[b][:, :], words.to_broadcast([P // 8, 8, UW])).then_inc(raw_in[b], 16)
                    sp.dma_start(sc[b][:, :], scales[u:u + 1, :].to_broadcast([P, UW])).then_inc(raw_in[b], 16)

                sp.dma_start(q_raw[:, :, :], cond_t).then_inc(scan_in, 16)
                sp.dma_start(bias[:, :], bias_t).then_inc(scan_in, 16)
                load_unit(0)
                for half in range(2):
                    sp.dma_start(dr[:, half * HS:(half + 1) * HS], drive[half]).then_inc(loaded, 16)
                load_unit(1)
                load_unit(2)
                sp.dma_start(coup[:, :, :], coupling_t).then_inc(coup_in, 16)
                for u in range(3, UNITS):
                    load_unit(u)
                sp.wait_ge(loaded, 32)

            @block.gpsimd
            def _(pool):
                nc.gpsimd.iota(shift[:, :], [[0, 1]], base=P - 1, channel_multiplier=-1).then_inc(iota_done, 1)
                for name, column in (("p", BY_P), ("q1", BY_Q1), ("q2", BY_Q2), ("q3", BY_Q3)):
                    for row in range(1, ROWS):
                        nc.gpsimd.memset(by[name][:, row], float(LINEAR[row, column]))
                nc.gpsimd.memset(mhalf[:, :], -0.5)
                for u in range(UNITS):
                    pool.wait_ge(dq_hi, u + 1)
                    nc.gpsimd.tensor_tensor(wffn[:, u, 1, :], w32[u % UNPACK_BUFS][:, :], wffn[:, u, 0, :],
                                            ALU.subtract).then_inc(dq_lo, 1)

            @block.scalar
            def _(act):
                nc.scalar.preload_act_table(ACT.Silu)
                act.wait_ge(loaded, 32)
                act.wait_ge(constants, ROWS)
                for n in range(SUM_R_PARTS):
                    sum_drive(n, 0, sums_set)
                for u in range(UNITS):
                    act.wait_ge(dq_w32, u + 1)
                    nc.scalar.activation(wffn[:, u, 0, :], w32[u % UNPACK_BUFS][:, :], ACT.Copy).then_inc(dq_hi, 1)
                    if u == 1:
                        act.wait_ge(coup_in, 16)
                        for n, coef in enumerate(COEF):
                            nc.scalar.activation(wscan[:, n, 0], coup[:, :, :], ACT.Copy,
                                                 scale=coef * S).then_inc(coup_hi, 1)

            @block.vector
            def _(dve):
                count = [0]

                def link(ins):
                    count[0] += 1
                    ins.then_inc(setup_link, 1)
                    dve.wait_ge(setup_link, count[0])

                dve.wait_ge(scan_in, 32)
                nc.vector.tensor_scalar(p_state[:, :, :], q_raw[:, :, :], S, None, ALU.mult)
                nc.vector.tensor_scalar(hist[:, :, STEPS - 1, :], q_raw[:, :, :], S, None, ALU.mult)
                for row in range(ROWS):
                    nc.vector.tensor_scalar(constant[:, row], bias[:, :], float(LINEAR[row, BY_R] * S),
                                            float(LINEAR[row, BY_ONE] * S), ALU.mult, ALU.add).then_inc(constants, 1)
                dve.wait_ge(constants, ROWS)
                for c in range(KT):
                    wide = constant[:, ROWS - 1, c:c + 1].unsqueeze(2).to_broadcast([P, STEPS, B])
                    nc.vector.tensor_copy(sum_r[:, :, ROWS - 1, c, :], wide)
                dve.wait_ge(iota_done, 1)
                link(nc.vector.tensor_scalar(shift[:, :], shift[:, :], 7, 2, ALU.bitwise_and,
                                             ALU.logical_shift_left))
                link(nc.vector.tensor_copy(q_raw[:, :, :], hist[:, :, STEPS - 1, :]))

                def unpack(u):
                    b = u % UNPACK_BUFS
                    bits = nib[u % 2]
                    dve.wait_ge(raw_in[b], 32 * (u // UNPACK_BUFS + 1))
                    link(nc.vector.tensor_scalar(bits[:, :], raw[b][:, :], shift[:, 0:1], -(1 << 28),
                                                 ALU.logical_shift_left, ALU.bitwise_and))
                    link(nc.vector.tensor_scalar(bits[:, :], bits[:, :], 3, 0x8E000000 - (1 << 32),
                                                 ALU.arith_shift_right, ALU.bitwise_and))
                    fp4 = bits[:, :].bitcast(F16).rearrange("p (n two) -> p n two", two=2)[:, :, 1]
                    if u >= UNPACK_BUFS:
                        dve.wait_ge(dq_lo, u - UNPACK_BUFS + 1)
                    nc.vector.scalar_tensor_tensor(w32[b][:, :], fp4, FP4_BITS * W_SCALE, sc[b][:, :],
                                                   ALU.mult, ALU.mult).then_inc(dq_w32, 1)

                for u in range(UNPACK_BUFS + 1):
                    unpack(u)
                dve.wait_ge(sums_set, SUM_R_PARTS)
                nc.vector.scalar_tensor_tensor(linear0[:, :, :], p_state[:, :, :], float(LINEAR[0, BY_P]),
                                               sum_r[:, 0, 0], ALU.mult, ALU.add)
                for n, coef in enumerate(COEF):
                    dve.wait_ge(coup_hi, n + 1)
                    nc.vector.scalar_tensor_tensor(wscan[:, n, 1], coup[:, :, :], coef * S, wscan[:, n, 0],
                                                   ALU.mult, ALU.subtract)
                for u in range(UNPACK_BUFS + 1, UNITS):
                    unpack(u)

        def jobs(now, before, ffn, rest, s):
            here = []
            if rest and STAGES + s < SCHEDULE.end:
                here.append((SCHEDULE, before, now, STAGES + s))
            if ffn:
                here.append((SCHEDULE, now, before, s) if rest else (FIRST_SCHEDULE, now, None, s))
            return here

        def sp_block(sp, k, now, before, ffn, rest):
            if before:
                sp.wait_ge(before.sum_r_ready, 2 * SUM_R_PARTS)
            sp.dma_start(dr[:, 0:HS], drive[2 * k + 2]).then_inc(now.drive_lo, 16)
            if rest:
                sp_store(sp, before, k - 2)
            if ffn:
                sp_residual(sp, now, k - 1)
            sp.wait_ge(now.sum_r_ready, SUM_R_PARTS)
            sp.dma_start(dr[:, HS:STEPS], drive[2 * k + 3]).then_inc(now.drive_hi, 16)

        def pe_block(pe, now, before, ffn, rest):
            def couple(s, part, k_half, n_half, tanh_parts=2):
                w, t_in = STAGE_COEF[s % 4], th[s % 2]
                for c in range(HC):
                    for kt in range(k_half * HC, (k_half + 1) * HC):
                        cols = slice((n_half * HC + c) * P, (n_half * HC + c + 1) * P)
                        to = prod[n_half][:, :, c * B:(c + 1) * B]
                        first = part == 1 and k_half == 0 and c == 0 and kt == 0
                        last = part == 0 and k_half == 1 and c == HC - 1 and kt == KT - 1
                        both = tanh_parts == 2
                        i = nc.tensor.matmul(to if both else to[:, 0], wscan[:, w, part, kt, cols],
                                             t_in[:, kt, :, :] if both else t_in[:, kt, 0, :],
                                             start=first, stop=last, skip_group_check=True)
                return i

            for s in range(STAGES):
                pe.wait_ge(now.tanh_hi, 2 * s + 1)
                couple(s, 1, 0, 0, 1)
                if s:
                    pe.wait_ge(now.q_ready, 2 * s)
                elif before:
                    pe.wait_ge(before.q_ready, 2 * STAGES)
                couple(s, 1, 0, 1, 1)
                pe.wait_ge(now.tanh_hi, 2 * s + 2)
                couple(s, 1, 1, 0, 1)
                pe.wait_ge(now.tanh_lo, 2 * s + 1)
                couple(s, 0, 0, 0)
                couple(s, 0, 0, 1)
                pe.wait_ge(now.tanh_lo, 2 * s + 2)
                couple(s, 0, 1, 0).then_inc(now.products, 1)
                couple(s, 1, 1, 1)
                couple(s, 0, 1, 1).then_inc(now.products, 1)
                for job in jobs(now, before, ffn, rest, s):
                    pe_ffn(pe, *job)

        def act_block(act, now, before, ffn, rest):
            for s in range(STAGES):
                q = q_raw if s % 4 == 0 else q_stage[s % 4 - 1]
                for half in range(2):
                    c = slice(half * HC, (half + 1) * HC)
                    if s:
                        act.wait_ge(now.q_ready, 2 * s - 1 + half)
                    elif before:
                        act.wait_ge(before.q_ready, 2 * STAGES - 1 + half)
                    nc.scalar.activation(th[s % 2][:, c, 0, :], q[:, c, :], ACT.Tanh,
                                         scale=1.0 / S).then_inc(now.tanh_hi, 1)
                    nc.scalar.activation(t32[:, c, :], q[:, c, :], ACT.Tanh,
                                         scale=1.0 / S).then_inc(now.tanh_32, 1)
                if ffn and s in (1, 2):
                    act.wait_ge(before.clipped, STEPS)
                    for c in range((s - 1) * HC, s * HC):
                        hist_high(act, now, c)
                if s == 1 and before:
                    act.wait_ge(before.drive_hi, 16)
                if s == 2 * SUM_R_PARTS:
                    act.wait_ge(now.drive_lo, 16)
                if s < 2 * SUM_R_PARTS and s % 2 == 1:
                    sum_drive(s // 2, 1, now.sum_r_ready)
                if s >= 2 * SUM_R_PARTS and s % 2 == 0:
                    sum_drive(s // 2 - SUM_R_PARTS, 0, now.sum_r_ready)
                for job in jobs(now, before, ffn, rest, s):
                    act_ffn(act, *job)

        def dve_block(dve, now, before, ffn, rest):
            linear = [linear0[:, :, :], sum_q1[:, 1], sum_q2[:, 2], sum_q3[:, 3]]
            for s in range(STAGES):
                t, i = divmod(s, 4)
                q = hist[:, :, (t - 1) % STEPS, :] if i == 0 else q_stage[i - 1][:, :, :]
                q_next = q_raw if i == 3 else q_stage[i]

                def square():
                    if i:
                        dve.wait_ge(now.q_ready, 2 * s)
                    elif t:
                        dve.wait_ge(now.clipped, t)
                    elif before:
                        dve.wait_ge(before.clipped, STEPS)
                    nc.vector.tensor_tensor(q_sq[:, :, :], q, q, ALU.mult).then_inc(now.squared, 1)

                def cube():
                    dve.wait_ge(now.squared, s + 1)
                    nc.vector.scalar_tensor_tensor(q_cub[:, :, :], q_sq[:, :, :], SHIFT[i], q,
                                                   ALU.add, ALU.mult).then_inc(now.cubed, 1)

                def low_part(half):
                    c = slice(half * HC, (half + 1) * HC)
                    dve.wait_ge(now.tanh_32, 2 * s + 1 + half)
                    nc.vector.tensor_tensor(th[s % 2][:, c, 1, :], t32[:, c, :], th[s % 2][:, c, 0, :],
                                            ALU.subtract).then_inc(now.tanh_lo, 1)

                if i:
                    square()
                    low_part(0)
                    cube()
                    low_part(1)
                else:
                    low_part(0)
                    square()
                    low_part(1)
                    cube()
                dve.wait_ge(now.cubed, s + 1)
                if i:
                    dve.wait_ge(now.pool_local, 3 * t + i)
                elif t:
                    dve.wait_ge(now.linear0, t)
                elif before:
                    dve.wait_ge(before.linear0, STEPS)
                nc.vector.scalar_tensor_tensor(local_ps, halves(q_cub[:, :, :]), CUBE[i], halves(linear[i]),
                                               ALU.mult, ALU.add).then_inc(now.local_in, 1)
                for job in jobs(now, before, ffn, rest, s):
                    dve_ffn(dve, *job)
                if ffn and s in (1, 2):
                    for c in range((s - 1) * HC, s * HC):
                        hist_low(dve, now, c)
                for half in range(2):
                    if half == 0 and i == 0:
                        dve.wait_ge(now.local_in, s + 1)
                    dve.wait_ge(now.products, 2 * s + 1 + half)
                    if half == 0 and i:
                        dve.wait_ge(now.local_in, s + 1)
                    nc.vector.tensor_reduce(q_next[:, half * HC:(half + 1) * HC, :], three[half], AX.X,
                                            ALU.add).then_inc(now.q_ready, 1)
                if i == 3:
                    dve.wait_ge(now.p_ready, t + 1)
                    if t + 1 == HS:
                        dve.wait_ge(now.sum_r_ready, SUM_R_PARTS)
                    if t + 1 == STEPS:
                        dve.wait_ge(now.sum_r_ready, 2 * SUM_R_PARTS)
                    nc.vector.scalar_tensor_tensor(linear0[:, :, :], p_state[:, :, :], float(LINEAR[0, BY_P]),
                                                   sum_r[:, (t + 1) % STEPS, 0], ALU.mult,
                                                   ALU.add).then_inc(now.linear0, 1)
                    dve.wait_ge(now.q_ready, 2 * s + 2)
                    if ffn and t == 0:
                        dve.wait_ge(now.xl_ready, KT)
                    nc.vector.tensor_scalar(hist[:, :, t, :], q_raw[:, :, :], -CLAMP * S, CLAMP * S,
                                            ALU.max, ALU.min).then_inc(now.clipped, 1)

        def pool_block(pool, now, before, ffn, rest):
            links, locals_done = [0], [0]

            def link(ins):
                links[0] += 1
                ins.then_inc(now.pool_link, 1)
                pool.wait_ge(now.pool_link, links[0])

            def to_dve(ins):
                locals_done[0] += 1
                ins.then_inc(now.pool_local, 1)
                pool.wait_ge(now.pool_local, locals_done[0])

            def add_times(to, x, name, base, first, signal):
                rows = slice(first, ROWS)
                wide = x.unsqueeze(1).to_broadcast([P, ROWS - first, KT, B])
                link(nc.gpsimd.tensor_tensor(term[:, rows], wide, by[name][:, rows], ALU.mult))
                signal(nc.gpsimd.tensor_tensor(to[:, rows], term[:, rows], base[:, rows], ALU.add))

            def ffn_part(s):
                for plan, f, _, at in jobs(now, before, ffn, rest, s):
                    if at == plan.norm_root:
                        norm_root(pool, f)

            for t in range(STEPS):
                if t == 0 and before:
                    pool.wait_ge(before.sum_r_ready, 2 * SUM_R_PARTS)
                if t == HS:
                    pool.wait_ge(now.sum_r_ready, SUM_R_PARTS)
                add_times(sum_p, p_state[:, :, :], "p", sum_r[:, t], 1, link)
                ffn_part(4 * t)
                if t:
                    pool.wait_ge(now.clipped, t)
                elif before:
                    pool.wait_ge(before.clipped, STEPS)
                add_times(sum_q1, hist[:, :, (t - 1) % STEPS, :], "q1", sum_p, 1, to_dve)
                ffn_part(4 * t + 1)
                pool.wait_ge(now.q_ready, 8 * t + 2)
                add_times(sum_q2, q_stage[0][:, :, :], "q2", sum_q1, 2, to_dve)
                ffn_part(4 * t + 2)
                pool.wait_ge(now.q_ready, 8 * t + 4)
                add_times(sum_q3, q_stage[1][:, :, :], "q3", sum_q2, 3, to_dve)
                ffn_part(4 * t + 3)
                pool.wait_ge(now.q_ready, 8 * t + 6)
                link(nc.gpsimd.tensor_scalar(p_term[:, :, :], q_stage[2][:, :, :], float(LINEAR[4, BY_Q4]), None,
                                             ALU.mult))
                link(nc.gpsimd.tensor_tensor(p_sum[:, :, :], p_term[:, :, :], sum_q3[:, 4], ALU.add))
                nc.gpsimd.tensor_scalar(p_state[:, :, :], p_sum[:, :, :], -CLAMP * S, CLAMP * S,
                                        ALU.max, ALU.min).then_inc(now.p_ready, 1)
                pool.wait_ge(now.p_ready, t + 1)
                if t == HS and before:
                    pool.wait_ge(now.xres_in, 16)
                    pool.wait_ge(now.down_done, 2)
                    pool.wait_ge(now.drive_lo, 16)
                    if rest:
                        pool.wait_ge(before.out_ready, KT)
                    nc.gpsimd.sem_clear(before.range)

        def sp_tail(sp, now, before):
            sp_store(sp, before, BLOCKS - 2)
            sp_residual(sp, now, BLOCKS - 1)
            sp_store(sp, now, BLOCKS - 1)
            sp.wait_ge(before.drive_hi, 16)

        def pe_tail(pe, now, before):
            for s in range(STAGES, SCHEDULE.end):
                pe_ffn(pe, SCHEDULE, before, now, s)
            for s in range(SCHEDULE.end):
                pe_ffn(pe, SCHEDULE, now, before, s)

        def act_tail(act, now, before):
            act.wait_ge(before.clipped, STEPS)
            for c in range(KT):
                hist_high(act, now, c)
            for s in range(STAGES, SCHEDULE.end):
                act_ffn(act, SCHEDULE, before, now, s)
            for s in range(SCHEDULE.end):
                act_ffn(act, SCHEDULE, now, before, s)

        def dve_tail(dve, now, before):
            for c in range(KT):
                hist_low(dve, now, c)
            for s in range(STAGES, SCHEDULE.end):
                dve_ffn(dve, SCHEDULE, before, now, s)
            for s in range(SCHEDULE.end):
                dve_ffn(dve, SCHEDULE, now, before, s)

        def pool_tail(pool, now, before):
            norm_root(pool, before)
            norm_root(pool, now)

        even, odd = signals
        with nc.Block() as block:
            @block.sync
            def _(sp):
                sp_block(sp, 0, even, None, ffn=False, rest=False)
                sp_block(sp, 1, odd, even, ffn=True, rest=False)
                with sp.Fori(1, BLOCKS // 2) as pair:
                    sp_block(sp, 2 * pair, even, odd, ffn=True, rest=True)
                    sp_block(sp, 2 * pair + 1, odd, even, ffn=True, rest=True)
                sp_tail(sp, even, odd)

            @block.tensor
            def _(pe):
                pe_block(pe, even, None, ffn=False, rest=False)
                pe_block(pe, odd, even, ffn=True, rest=False)
                with pe.Fori(1, BLOCKS // 2):
                    pe_block(pe, even, odd, ffn=True, rest=True)
                    pe_block(pe, odd, even, ffn=True, rest=True)
                pe_tail(pe, even, odd)

            @block.scalar
            def _(act):
                act_block(act, even, None, ffn=False, rest=False)
                act_block(act, odd, even, ffn=True, rest=False)
                with act.Fori(1, BLOCKS // 2):
                    act_block(act, even, odd, ffn=True, rest=True)
                    act_block(act, odd, even, ffn=True, rest=True)
                act_tail(act, even, odd)

            @block.vector
            def _(dve):
                dve_block(dve, even, None, ffn=False, rest=False)
                dve_block(dve, odd, even, ffn=True, rest=False)
                with dve.Fori(1, BLOCKS // 2):
                    dve_block(dve, even, odd, ffn=True, rest=True)
                    dve_block(dve, odd, even, ffn=True, rest=True)
                dve_tail(dve, even, odd)

            @block.gpsimd
            def _(pool):
                pool_block(pool, even, None, ffn=False, rest=False)
                pool_block(pool, odd, even, ffn=True, rest=False)
                with pool.Fori(1, BLOCKS // 2):
                    pool_block(pool, even, odd, ffn=True, rest=True)
                    pool_block(pool, odd, even, ffn=True, rest=True)
                pool_tail(pool, even, odd)


def kernel(x, cond_2048, L0_cond_coupling, L0_cond_bias, L0_ffn_gate_up_packed, L0_ffn_gate_up_scales,
           L0_ffn_down_packed, L0_ffn_down_scales):
    import concourse.bacc as bacc
    from concourse.bass_utils import run_bass_kernel_spmd

    x = np.asarray(x)
    drive = x.reshape(B, 2 * BLOCKS, HS, KT, P).transpose(1, 4, 2, 3, 0)
    drive = np.concatenate([drive, drive[-2:]])
    gu = np.asarray(L0_ffn_gate_up_packed).reshape(2, UNITS, P, KT, P // 8).transpose(1, 4, 0, 3, 2)
    dn = np.asarray(L0_ffn_down_packed).reshape(N, UNITS, P // 8).transpose(1, 2, 0)
    packed = np.concatenate([gu.reshape(UNITS, P // 8, 2 * KT * P), dn], axis=2)
    gus = np.asarray(L0_ffn_gate_up_scales).reshape(KT, 2, UNITS, P).transpose(2, 1, 0, 3)
    scales = np.concatenate([gus.reshape(UNITS, 2 * KT * P), np.asarray(L0_ffn_down_scales)], axis=1)
    arrays = {
        "x": x,
        "drive": drive,
        "cond_t": np.asarray(cond_2048).reshape(B, KT, P).transpose(2, 1, 0),
        "coupling_t": np.asarray(L0_cond_coupling).reshape(N, KT, P).transpose(2, 1, 0),
        "bias_t": np.asarray(L0_cond_bias).reshape(KT, P).T,
        "packed": packed,
        "scales": scales,
    }
    arrays = {name: np.ascontiguousarray(a) for name, a in arrays.items()}
    nc = bacc.Bacc("TRN2", target_bir_lowering=False, num_devices=1)
    args = [nc.dram_tensor(name, a.shape, mybir.dt.from_np(a.dtype), kind="ExternalInput").ap()
            for name, a in arrays.items()]
    out = nc.dram_tensor("out", (B, T, N), F32, kind="ExternalOutput").ap()
    program(nc, *args, out)
    r = run_bass_kernel_spmd(nc, [arrays], core_ids=[0])
    return r.results[0]["out"]
```
